# Optimizing a Trainium2 kernel written in Bass

```python
import numpy as np
import jax
import jax.numpy as jnp

def _softmax(x, axis=-1):
    return jax.nn.softmax(x, axis=axis)

def _gelu(x):
    return jax.nn.gelu(x, approximate=True)

def _silu(x):
    return jax.nn.silu(x)

def _sigmoid(x):
    return jax.nn.sigmoid(x)

def _layernorm(x, axis=-1, eps=1e-05):
    m = jnp.mean(x, axis=axis, keepdims=True)
    v = jnp.var(x, axis=axis, keepdims=True)
    return (x - m) / jnp.sqrt(v + eps)

def _scatter_add(tgt, idx, src, axis=0):
    return tgt.at[idx].add(src)

def _segment_sum(src, seg, n):
    return jax.ops.segment_sum(src, seg, n)
kernel_name = 'mk_lm_tower_d1_tok_ids2048_r4_bf061e'

def setup_inputs(seed: int=0):
    np.random.seed(seed)
    _w = jnp.asarray

    def _rec_inputs():
        import jax
        import jax.numpy as jnp
        _rk = jax.random.key(seed)
        x = jax.random.randint(jax.random.fold_in(_rk, 1), (8, 1024), 0, 127998, jnp.int32)
        return x
    x = _rec_inputs()

    def _L0_tok_setup():
        import jax, jax.numpy as jnp
        import numpy as np
        VOCAB = 32000
        DIM = 512
        N_TRAIN = 64
        BATCH, SEQ = (4, 1024)
        key = jax.random.key(seed)
        k1, k2, k3, k4 = jax.random.split(key, 4)
        x = jax.random.randint(k1, (BATCH, SEQ), 0, VOCAB, dtype=jnp.int64)
        W = jax.random.normal(k2, (VOCAB, DIM), dtype=jnp.float32)
        delta = jax.random.uniform(k3, (N_TRAIN * DIM,), dtype=jnp.float32)
        token_indices = jax.random.randint(k4, (N_TRAIN,), 0, VOCAB, dtype=jnp.int64)
        return {'x': x, 'W': W, 'delta': delta, 'token_indices': token_indices}
    _L0_tok_all = _L0_tok_setup()
    _L0_tok_in = {k: v for k, v in _L0_tok_all.items() if k in ('W', 'delta', 'token_indices')}
    del _L0_tok_all

    def _L0_attn_setup():
        import jax, jax.numpy as jnp
        import numpy as np
        B, L, DM, H, N = (4, 1024, 512, 32, 128)
        HD = DM // H
        key = jax.random.key(seed)
        ks = jax.random.split(key, 6)
        x = jax.random.normal(ks[0], (B, L, DM), dtype=jnp.float32)
        Wx = jax.random.normal(ks[1], (DM, 2 * N + H), dtype=jnp.float32) * 0.02
        Wg = jax.random.normal(ks[2], (DM, DM), dtype=jnp.float32) * 0.02
        bg = jnp.zeros((DM,), dtype=jnp.float32)
        Wo = jax.random.normal(ks[3], (DM, DM), dtype=jnp.float32) * 0.02
        A = -1.0 + 0.1 * jax.random.normal(ks[4], (H, N), dtype=jnp.float32)
        Dp = jnp.ones((H,), dtype=jnp.float32)
        return {'x': x, 'Wx': Wx, 'Wg': Wg, 'bg': bg, 'Wo': Wo, 'A': A, 'Dp': Dp}
    _L0_attn_all = _L0_attn_setup()
    _L0_attn_in = {k: v for k, v in _L0_attn_all.items() if k in ('Wx', 'Wg', 'bg', 'Wo', 'A', 'Dp')}
    del _L0_attn_all

    def _L0_ffn_setup():
        import jax, jax.numpy as jnp
        import numpy as np
        B, S, D = (4, 1024, 512)
        DFF = 4 * D
        SKIP = 0.125
        key = jax.random.key(seed)
        ks = jax.random.split(key, 4)
        s_in = 1.0 / np.sqrt(D).astype(np.float32)
        s_ff = 1.0 / np.sqrt(DFF).astype(np.float32)
        return {'x': jax.random.normal(ks[0], (B, S, D), jnp.float32), 'Wr': jax.random.normal(ks[1], (D, 1), jnp.float32) * s_in, 'br': jnp.zeros((1,), jnp.float32), 'W1': jax.random.normal(ks[2], (D, DFF), jnp.float32) * s_in, 'b1': jnp.zeros((DFF,), jnp.float32), 'W2': jax.random.normal(ks[3], (DFF, D), jnp.float32) * s_ff, 'b2': jnp.zeros((D,), jnp.float32)}
    _L0_ffn_all = _L0_ffn_setup()
    _L0_ffn_in = {k: v for k, v in _L0_ffn_all.items() if k in ('Wr', 'br', 'W1', 'b1', 'W2', 'b2')}
    del _L0_ffn_all
    return {'x': x, 'L0_tok_W': _L0_tok_in['W'], 'L0_tok_delta': _L0_tok_in['delta'], 'L0_tok_token_indices': _L0_tok_in['token_indices'], 'L0_attn_Wx': _L0_attn_in['Wx'], 'L0_attn_Wg': _L0_attn_in['Wg'], 'L0_attn_bg': _L0_attn_in['bg'], 'L0_attn_Wo': _L0_attn_in['Wo'], 'L0_attn_A': _L0_attn_in['A'], 'L0_attn_Dp': _L0_attn_in['Dp'], 'L0_ffn_Wr': _L0_ffn_in['Wr'], 'L0_ffn_br': _L0_ffn_in['br'], 'L0_ffn_W1': _L0_ffn_in['W1'], 'L0_ffn_b1': _L0_ffn_in['b1'], 'L0_ffn_W2': _L0_ffn_in['W2'], 'L0_ffn_b2': _L0_ffn_in['b2']}

def reference(x, L0_tok_W, L0_tok_delta, L0_tok_token_indices, L0_attn_Wx, L0_attn_Wg, L0_attn_bg, L0_attn_Wo, L0_attn_A, L0_attn_Dp, L0_ffn_Wr, L0_ffn_br, L0_ffn_W1, L0_ffn_b1, L0_ffn_W2, L0_ffn_b2):
    import jax
    import jax.numpy as jnp

    def _L0_tok_ref(x, W, delta, token_indices):
        import jax, jax.numpy as jnp
        import numpy as np
        VOCAB = 32000
        DIM = 512
        N_TRAIN = 64
        BATCH, SEQ = (4, 1024)
        delta_rows = delta.reshape(DIM, N_TRAIN).T
        W_adapted = W.at[token_indices].add(delta_rows)
        return W_adapted[x]

    def _L0_attn_ref(x, Wx, Wg, bg, Wo, A, Dp):
        import jax, jax.numpy as jnp
        import numpy as np
        B, L, DM, H, N = (4, 1024, 512, 32, 128)
        HD = DM // H
        b, l, dm = x.shape
        h, n = A.shape
        hd = dm // h
        ssm_params = x @ Wx
        B_ssm = ssm_params[..., :n]
        C_ssm = ssm_params[..., n:2 * n]
        delta_bias = ssm_params[..., 2 * n:]
        gate = jax.nn.sigmoid(x @ Wg + bg)
        delta = jax.nn.softplus(delta_bias[..., :, None] + B_ssm[..., None, :])
        d_seq = jnp.moveaxis(delta, 1, 0)
        h0 = jnp.zeros((b, h, n), dtype=x.dtype)

        def step(hst, d_t):
            hst = jnp.exp(d_t * A) * hst + d_t * d_t
            return (hst, hst)
        _, hs = jax.lax.scan(step, h0, d_seq)
        hs = jnp.moveaxis(hs, 0, 1)
        y = jnp.einsum('blhn,bln->blh', hs, C_ssm)
        xg = x.reshape(b, l, h, hd)
        yh = y[..., None] + xg * Dp[None, None, :, None]
        y_full = yh.reshape(b, l, dm) * gate
        return y_full @ Wo

    def _L0_ffn_ref(x, Wr, br, W1, b1, W2, b2):
        import jax, jax.numpy as jnp
        import numpy as np
        B, S, D = (4, 1024, 512)
        DFF = 4 * D
        SKIP = 0.125
        Bs, Ss, Ds = x.shape
        k = max(int(Ss * SKIP), 1)
        logits = (x @ Wr + br)[..., 0]
        weights, idx = jax.lax.top_k(logits, k)
        perm = jnp.argsort(idx, axis=1)
        tokens = jnp.take_along_axis(idx, perm, axis=1)
        fx = jnp.take_along_axis(x, tokens[..., None], axis=1)
        h = jax.nn.gelu(fx @ W1 + b1, approximate=False)
        out_l = h @ W2 + b2
        tw = jax.nn.softmax(weights, axis=1)
        rw = jnp.take_along_axis(tw, perm, axis=1)
        xw = rw[..., None] * out_l
        bidx = jnp.arange(Bs)[:, None]
        return x.at[bidx, tokens].add(xw)
    h = _L0_tok_ref(x, L0_tok_W, L0_tok_delta, L0_tok_token_indices)
    h = h + _L0_attn_ref(_layernorm(h, axis=-1), L0_attn_Wx, L0_attn_Wg, L0_attn_bg, L0_attn_Wo, L0_attn_A, L0_attn_Dp)
    h = h + _L0_ffn_ref(_layernorm(h, axis=-1), L0_ffn_Wr, L0_ffn_br, L0_ffn_W1, L0_ffn_b1, L0_ffn_W2, L0_ffn_b2)
    return h

_drawn_inputs = setup_inputs


def setup_inputs(seed=0):
    import zlib

    import numpy as np

    out = dict(_drawn_inputs(seed))
    spreads = {'L0_attn_bg': (0.0, 0.1),
     'L0_attn_Dp': (1.0, 0.2),
     'L0_ffn_b1': (0.0, 0.8),
     'L0_ffn_b2': (0.0, 2.0)}
    factors = {'L0_tok_delta': 26.425, 'L0_ffn_Wr': 8.0, 'L0_ffn_W1': 8.0, 'L0_ffn_W2': 8.0}
    for name, (base, spread) in spreads.items():
        noise = np.random.default_rng([zlib.crc32(name.encode()), seed]).standard_normal(out[name].shape)
        drawn = base * np.exp(spread * noise) if base else spread * noise
        out[name] = jnp.asarray(drawn.astype(out[name].dtype))
    for name, factor in factors.items():
        out[name] = (out[name] * factor).astype(out[name].dtype)
    return out
```

```python
import concourse.bass as bass
from concourse import mybir
from contextlib import ExitStack

F32 = mybir.dt.float32
F32R = mybir.dt.float32r
I32 = mybir.dt.int32
ALU = mybir.AluOpType
ACT = mybir.ActivationFunctionType
AX = mybir.AxisListType

P = 128
B, L, DM = 8, 1024, 512
H, N = 32, 128
HD = DM // H
VOCAB, TRAIN = 32000, 64
DFF = 4 * DM
KEEP = L // 8
KC = DM // P
TILES = L // P
FT = DFF // P
PROJ = 2 * N + 2 * H
EPS = 1e-5
BIG = float(2 ** 62)
GROUP = 4
GROUPS = H // GROUP
BLK = 32
USLOTS, ASLOTS = 4, 2
CHUNKS = 16
HALF = CHUNKS // 2
NATURAL_LOG_EXP = "natural_log_exp_and_others"

def pre_step(t):
    return 5 + 5 * t // 2

def post_step(t):
    return 6 + 3 * t

FFN_STEP = 24


def build(nc, ids, W, delta_t, train_row, train_col, Wx, Wg, bg, Wo, A_t, Dp, Wr, br, W1, b1_t, W2, b2, out):
    xs_dram = nc.dram_tensor("normed2", [L, DM], F32, kind="Internal").ap()
    gate_dram = nc.dram_tensor("gates", [B * L, DM], F32, kind="Internal").ap()
    xg_dram = nc.dram_tensor("gated_skip", [B * L, DM], F32, kind="Internal").ap()
    h0_dram = nc.dram_tensor("embedded", [B * L, DM], F32, kind="Internal").ap()
    adapted_dram = nc.dram_tensor("adapted", [TRAIN, DM], F32, kind="Internal").ap()

    ctx = ExitStack()
    with ctx:
        def sb(name, shape, dt=F32):
            return ctx.enter_context(nc.sbuf_tensor(name, shape, dt))

        def sem(name):
            return ctx.enter_context(nc.semaphore(name))

        ident = sb("ident", [P, P])
        slot_iota = sb("slot_iota", [P, P])
        before = sb("before", [P, P])
        ones = sb("ones", [P, P])
        ones_r = sb("ones_r", [2 * BLK, P], F32R)
        diag32 = sb("diag32", [P, BLK])
        head_sel = sb("head_sel", [2 * H, H], F32R)
        dp_row = sb("dp_row", [P, DM])
        wr_row = sb("wr_row", [P, DM])
        b2_row = sb("b2_row", [P, DM])
        bias_g = sb("bias_g", [2 * BLK, DM], F32R)
        a_t = sb("a_t", [N, H])
        b1s = sb("b1s", [P, FT])
        small = sb("small", [P, 48])
        eps_c, br_c = small[:, 0:1], small[:, 1:2]
        wx_hi, wx_lo = sb("wx_hi", [P, KC, PROJ], F32R), sb("wx_lo", [P, KC, PROJ], F32R)
        wg_hi, wg_lo = sb("wg_hi", [P, KC, DM], F32R), sb("wg_lo", [P, KC, DM], F32R)
        wo_hi, wo_lo = sb("wo_hi", [P, KC, DM], F32R), sb("wo_lo", [P, KC, DM], F32R)
        ffn_w = sb("ffn_w", [P, 2, 1024])
        id_f, id_i = sb("id_f", [P, B * TILES]), sb("id_i", [P, B * TILES], I32)
        row_i = sb("row_i", [P, B * TILES], I32)
        id_now, row_now = sb("id_now", [P, TILES], I32), sb("row_now", [P, TILES], I32)
        token_no = sb("token_no", [P, TILES])
        br_raw, c_raw, db_raw = sb("b_raw", [N, L]), sb("c_raw", [N, L]), sb("db_raw", [2 * H, L])
        eb, cc, edb = sb("exp_b", [N, L]), sb("c_now", [N, L]), sb("exp_db", [2 * H, L], F32R)
        u = sb("u", [N, USLOTS, L])
        a = sb("decay", [N, ASLOTS, L])
        x = sb("states", [N, 2, GROUP, L])
        picked = sb("picked", [P, TILES * P])
        y_next, y_now = sb("y_next", [P, TILES, H]), sb("y_now", [P, TILES, H])
        emb = sb("emb", [P, 4, DM])
        xn = sb("xn", [P, 2, DM])
        xt_hi, xt_lo = sb("xt_hi", [P, KC, P], F32R), sb("xt_lo", [P, KC, P], F32R)
        gate = sb("gate", [P, 2, DM])
        stats, mv, rstd = sb("stats", [P, 4, 6]), sb("mv", [P, 4, 2]), sb("rstd", [P, 4])
        q_gate, q_xg, q_h = sb("q_gate", [P, 2, DM]), sb("q_xg", [P, 1, DM]), sb("q_h", [P, 2, DM])
        yt_hi, yt_lo = sb("yt_hi", [P, KC, P], F32R), sb("yt_lo", [P, KC, P], F32R)
        x2 = sb("x2", [P, 2, DM])
        stats2, mv2, rstd2 = sb("stats2", [P, 2, 6]), sb("mv2", [P, 2, 2]), sb("rstd2", [P, 2])
        logit = sb("logit", [P, TILES])
        rank = sb("rank", [P, 8, TILES])
        weigh = sb("weigh", [P, 4, TILES])
        slot_rhs = sb("slot_rhs", [P, TILES, 4])
        idx, idx_out = sb("idx", [P, 2], I32), sb("idx_out", [P, 1], I32)
        slot_w, slot_w_now = sb("slot_w", [P, 1]), sb("slot_w_now", [P, 1])
        fx, fxt = sb("fx", [P, DM]), sb("fxt", [P, KC, P])
        hid = sb("hid", [P, FT, P])
        one_hot = sb("one_hot", [P, TILES, P])
        logit_row = picked[:, :].rearrange("p (t c) -> p t c", c=P)

        ps_e = ctx.enter_context(nc.psum_tensor("ps_e", [P, 2, L], F32))
        ps_y = ctx.enter_context(nc.psum_tensor("ps_y", [P, TILES * P], F32))
        ps_a = ctx.enter_context(nc.psum_tensor("ps_a", [P, DM], F32))
        ps_b = ctx.enter_context(nc.psum_tensor("ps_b", [P, DM], F32))

        s_passed = {nc.sync.engine: sem("sp_passed"), nc.gpsimd.engine: sem("pool_passed"), nc.vector.engine: sem("dve_passed")}
        s_const, s_ids, s_stage, s_wload = sem("const_loaded"), sem("ids_loaded"), sem("table_built"), sem("weights_loaded")
        s_iota, s_zero, s_setup, s_split = sem("iota_done"), sem("zero_done"), sem("setup_done"), sem("split_done")
        s_tm, s_ta = sem("table_mm"), sem("table_stored")
        s_eb, s_cc, s_dbx, s_dbh, s_edb = sem("eb_ready"), sem("cc_ready"), sem("db_exp"), sem("db_hi"), sem("edb_ready")
        s_bc, s_u, s_d, s_a, s_x = sem("bcast_done"), sem("u_ready"), sem("d_ready"), sem("a_ready"), sem("x_ready")
        s_scan, s_y, s_pick, s_yr, s_yn = sem("scan_done"), sem("contracted"), sem("picked_ready"), sem("y_ready"), sem("y_now_ready")
        s_idn = sem("ids_now")
        s_g1, s_g2 = [sem("rows_even"), sem("rows_odd")], [sem("adapted_even"), sem("adapted_odd")]
        s_st, s_mv, s_ln, s_rs, s_xn = sem("stats_ready"), sem("mv_ready"), sem("lnv_ready"), sem("rstd_ready"), sem("xn_ready")
        s_pt, s_xth, s_xtl, s_pp, s_pe = sem("pre_t"), sem("xt_hi_ready"), sem("xt_lo_ready"), sem("pre_proj"), sem("pre_evac")
        s_pg, s_ge, s_gm, s_gl, s_gr = sem("gate_mm"), sem("gate_exp"), sem("gate_min"), sem("gate_ln"), sem("gate_ready")
        s_xd, s_xg = sem("xd_ready"), sem("xg_ready")
        s_spill = [sem("spill_even"), sem("spill_odd")]
        s_qh = [sem("post_h_even"), sem("post_h_odd")]
        s_ql, s_qx = [sem("post_load_even"), sem("post_load_odd")], sem("post_load_xg")
        s_ym, s_yf, s_qt, s_yth, s_ytl = sem("y_gated"), sem("y_full"), sem("post_t"), sem("yt_hi_ready"), sem("yt_lo_ready")
        s_wo, s_h1, s_st2, s_mv2, s_ln2, s_rs2 = sem("wo_done"), sem("h1_ready"), sem("stats2_ready"), sem("mv2_ready"), sem("lnv2_ready"), sem("rstd2_ready")
        s_x2, s_lg, s_base = sem("x2_ready"), sem("logit_ready"), sem("base_ready")
        s_store = [sem("store_even"), sem("store_odd")]
        s_dg, s_lb, s_lr = sem("diag_ready"), sem("logit_bcast"), sem("logit_row_ready")
        s_r, s_rmax, s_re, s_es, s_z, s_rv, s_oh, s_sl, s_ix, s_tok = (
            sem("rank_chain"), sem("row_max"), sem("row_exp"), sem("exp_sum"), sem("z_done"), sem("slot_rhs_ready"),
            sem("one_hot_ready"), sem("slots_done"), sem("idx_ready"), sem("token_no_next"))
        s_fx,  s_ic, s_ft, s_fxt = sem("fx_loaded"), sem("idx_copied"), sem("fx_t"), sem("fxt_ready")
        s_w = [sem("chunk_even"), sem("chunk_odd")]
        s_ff, s_hc, s_gelu, s_ol, s_fo, s_sc = sem("chunk_used"), sem("hid_copied"), sem("gelu_done"), sem("ffn_sum"), sem("ffn_out"), sem("scattered")

        block = ctx.enter_context(nc.Block())

        def wait(eng, s, value):
            if not isinstance(value, int) or value > 0:
                eng.wait_ge(s, value)

        def plain(eng, b):
            if not isinstance(b, int):
                eng.sem_inc(s_passed[eng.engine], 1)

        def passes(eng, one):
            one(-1, pre=True)
            one(0, pre=True, ssm=True)
            one(1, pre=True, ssm=True, before=True, post=True)
            with eng.Fori(2, B - 1) as b:
                one(b, pre=True, ssm=True, before=True, post=True, ffn=True)
            one(B - 1, ssm=True, before=True, post=True, ffn=True)
            one(B, before=True, post=True, ffn=True)
            one(B + 1, ffn=True)

        def rows(b, t):
            return bass.ds(b * L + t * P, P)

        @block.sync
        def _(sp):
            sp.dma_start(id_i[:, :], ids).then_inc(s_ids, 16)
            sp.dma_start(row_i[:, 0:TRAIN], train_row.partition_broadcast(P)).then_inc(s_ids, 16)
            sp.dma_start(id_now[0:TRAIN, 0:1], train_col).then_inc(s_ids, 16)
            sp.dma_start(picked[0:TRAIN, 0:DM], delta_t).then_inc(s_const, 16)
            sp.dma_start(dp_row[:, 0:H], Dp.partition_broadcast(P)).then_inc(s_const, 16)
            sp.dma_start(wr_row[:, :], Wr.partition_broadcast(P)).then_inc(s_const, 16)
            sp.dma_start(b2_row[:, :], b2.partition_broadcast(P)).then_inc(s_const, 16)
            sp.dma_start(a_t[:, :], A_t).then_inc(s_const, 16)
            sp.dma_start(b1s[:, :], b1_t).then_inc(s_const, 16)
            sp.dma_start(br_c, br.partition_broadcast(P)).then_inc(s_const, 16)
            sp.dma_start(q_gate[0:1, 0, :], bg).then_inc(s_const, 16)
            sp.dma_start(q_gate[BLK:BLK + 1, 0, :], bg).then_inc(s_const, 16)
            wx_v = Wx.rearrange("(k p) n -> p k n", p=P)
            stage = x[:, 0, :, :].rearrange("p a b -> p (a b)")
            wx_st = stage[:, 0:KC * PROJ].rearrange("p (k n) -> p k n", k=KC)
            sp.dma_start(wx_st[:, :, 0:2 * N + H], wx_v).then_inc(s_wload, 16)
            sp.dma_start(wx_st[:, :, 2 * N + H:PROJ], wx_v[:, :, 2 * N:2 * N + H]).then_inc(s_wload, 16)
            sp.dma_start(x[:, 1, 0:2, :].rearrange("p a (b n) -> p (a b) n", n=DM),
                         Wg.rearrange("(k p) n -> p k n", p=P)).then_inc(s_wload, 16)
            sp.dma_start(x[:, 1, 2:4, :].rearrange("p a (b n) -> p (a b) n", n=DM),
                         Wo.rearrange("(k p) n -> p k n", p=P)).then_inc(s_wload, 16)
            sp.wait_ge(s_stage, 1)
            sp.dma_start(adapted_dram, picked[0:TRAIN, DM:2 * DM]).then_inc(s_ta, 16)

            w1_v = W1.rearrange("(k p) n -> p k n", p=P)
            w2_v = W2.rearrange("(f p) n -> p f n", p=P)

            def weights(b, c):
                if c < 2:
                    wait(sp, s_fo, b + 1)
                else:
                    wait(sp, s_ff, CHUNKS * b + c - 1)
                dst = ffn_w[:, c % 2, :]
                if c < HALF:
                    sp.dma_start(dst.rearrange("p (k n) -> p k n", k=KC), w1_v[:, :, 256 * c:256 * c + 256])\
                      .then_inc(s_w[c % 2], 16)
                else:
                    f = 2 * (c - HALF)
                    sp.dma_start(dst.rearrange("p (f n) -> p f n", f=2), w2_v[:, f:f + 2, :])\
                      .then_inc(s_w[c % 2], 16)

            def one(b, pre=False, ssm=False, before=False, post=False, ffn=False):
                if ffn:
                    weights(b - 2, 0)
                    weights(b - 2, 1)
                for h in range(H):
                    for t in range(TILES):
                        if pre and h == pre_step(t) + 3:
                            n = 4 * (b + 1) + t // 2
                            wait(sp, s_xg, TILES * (b + 1) + t + 1)
                            wait(sp, s_spill[t % 2], 48 * n)
                            s = s_spill[t % 2]
                            sp.dma_start(gate_dram[rows(b + 1, t), :], gate[:, t % 2, :]).then_inc(s, 16)
                            sp.dma_start(xg_dram[rows(b + 1, t), :], xn[:, t % 2, :]).then_inc(s, 16)
                            sp.dma_start(h0_dram[rows(b + 1, t), :], emb[:, t % 4, :]).then_inc(s, 16)
                        if post and h == post_step(t) - 3:
                            n = TILES * (b - 1) + t
                            wait(sp, s_spill[t % 2], 48 * (4 * (b - 1) + t // 2 + 1))
                            plain(sp, b)
                            wait(sp, s_yf, n)
                            plain(sp, b)
                            wait(sp, s_qt, n - 1)
                            plain(sp, b)
                            sp.dma_start(q_xg[:, 0, :], xg_dram[rows(b - 1, t), :]).then_inc(s_qx, 16)
                            sp.dma_start(q_gate[:, t % 2, :], gate_dram[rows(b - 1, t), :]).then_inc(s_ql[t % 2], 16)
                        if post and h == post_step(t) - 1:
                            wait(sp, s_store[t % 2], 32 * (4 * (b - 1) + t // 2))
                            plain(sp, b)
                            sp.dma_start(q_h[:, t % 2, :], h0_dram[rows(b - 1, t), :]).then_inc(s_qh[t % 2], 16)
                        if post and h == min(post_step(t) + 4, H - 1):
                            n = TILES * (b - 1) + t
                            if t == 0:
                                wait(sp, s_fx, 16 * (b - 1))
                            wait(sp, s_x2, n + 1)
                            sp.dma_start(xs_dram[P * t:P * t + P, :], x2[:, t % 2, :]).then_inc(s_store[t % 2], 16)
                            wait(sp, s_base, n + 1)
                            sp.dma_start(out[rows(b - 1, t), :], q_h[:, t % 2, :]).then_inc(s_store[t % 2], 16)
                    if ffn and FFN_STEP <= h < FFN_STEP + 7:
                        weights(b - 2, 2 * (h - FFN_STEP) + 2)
                        weights(b - 2, 2 * (h - FFN_STEP) + 3)

            passes(sp, one)
            sp.wait_ge(s_sc, 16 * (B + 1))
            for s in s_store:
                sp.wait_ge(s, 32 * 4 * B)

        @block.gpsimd
        def _(pool):
            pool.memset(ident[:, :], 0.0).then_inc(s_zero, 1)
            pool.memset(ones[:, :], 1.0).then_inc(s_zero, 1)
            pool.wait_ge(s_zero, 2)
            pool.affine_select(out=ident[:, :], in_=ident[:, :], compare_op=ALU.not_equal, fill=1.0, base=0,
                               pattern=[[-1, P]], channel_multiplier=1).then_inc(s_iota, 1)
            pool.affine_select(out=before[:, :], in_=ones[:, :], compare_op=ALU.is_gt, fill=0.0, base=0,
                               pattern=[[-1, P]], channel_multiplier=1).then_inc(s_iota, 1)
            pool.iota(slot_iota[:, :], pattern=[[1, P]], base=0, channel_multiplier=0,
                      allow_small_or_imprecise_dtypes=True).then_inc(s_iota, 1)
            pool.iota(token_no[:, :], pattern=[[P, TILES]], base=0, channel_multiplier=1,
                      allow_small_or_imprecise_dtypes=True).then_inc(s_iota, 1)
            pool.wait_ge(s_setup, 1)
            pool.indirect_dma_start(u[0:TRAIN, 3, 0:DM], None, W,
                                    bass.IndirectOffsetOnAxis(id_now[0:TRAIN, 0:1], 0)).then_inc(s_sc, 16)
            pool.wait_ge(s_setup, 3)
            pool.wait_ge(s_stage, 1)
            pool.wait_ge(s_ta, 16)

            def gather(b, p):
                wait(pool, s_spill[0], 48 * (4 * b + p - 1))
                wait(pool, s_spill[1], 48 * (4 * b + p - 1))
                plain(pool, b)
                for t in (2 * p, 2 * p + 1):
                    pool.indirect_dma_start(emb[:, t % 4, :], None, W,
                                            bass.IndirectOffsetOnAxis(id_now[:, t:t + 1], 0)).then_inc(s_g1[p % 2], 16)

            def overlay(b, p):
                wait(pool, s_g1[p % 2], 32 * (2 * b + p // 2 + 1))
                plain(pool, b)
                for t in (2 * p, 2 * p + 1):
                    pool.indirect_dma_start(emb[:, t % 4, :], None, adapted_dram,
                                            bass.IndirectOffsetOnAxis(row_now[:, t:t + 1], 0),
                                            bounds_check=TRAIN - 1, oob_is_err=False).then_inc(s_g2[p % 2], 16)

            def one(b, pre=False, ssm=False, before=False, post=False, ffn=False):
                if pre:
                    wait(pool, s_g2[1], 32 * 2 * (b + 1))
                    wait(pool, s_g2[0], 32 * 2 * (b + 1))
                    plain(pool, b)
                    col = bass.ds((b + 1) * TILES, TILES)
                    pool.tensor_copy(id_now[:, :], id_i[:, col]).then_inc(s_idn, 1)
                    pool.tensor_copy(row_now[:, :], row_i[:, col]).then_inc(s_idn, 1)
                    pool.wait_ge(s_idn, 2 * (b + 1) + 2)
                for h in range(H):
                    if ssm:
                        i = H * b + h
                        wait(pool, s_d, i + 1)
                        if h % GROUP == 0:
                            wait(pool, s_y, GROUPS * b + h // GROUP - 1)
                        pool.tensor_tensor(x[:, h // GROUP % 2, h % GROUP, :], u[:, h % USLOTS, :], u[:, h % USLOTS, :],
                                           ALU.mult).then_inc(s_x, 1)
                    if pre:
                        for p in range(TILES // 2):
                            if h == 5 * p + 1:
                                gather(b + 1, p)
                            if h == 5 * p + 2:
                                overlay(b + 1, p)
                        for t in range(TILES):
                            n = TILES * (b + 1) + t
                            if h == pre_step(t) + 1:
                                wait(pool, s_pt, n + 1)
                                pool.tensor_tensor(xn[:, t % 2, :], xn[:, t % 2, :], dp_row[:, :], ALU.mult).then_inc(s_xd, 1)
                            if h == pre_step(t) + 3:
                                wait(pool, s_gr, n + 1)
                                wait(pool, s_xd, n + 1)
                                pool.tensor_tensor(xn[:, t % 2, :], xn[:, t % 2, :], gate[:, t % 2, :], ALU.mult).then_inc(s_xg, 1)
                    if post and h == 5:
                        wait(pool, s_yr, GROUPS * b)
                        wait(pool, s_ym, TILES * (b - 1))
                        plain(pool, b)
                        pool.tensor_copy(y_now[:, :, :], y_next[:, :, :]).then_inc(s_yn, 1)
                    if post:
                        for t in range(TILES):
                            n = TILES * (b - 1) + t
                            half = 4 * (b - 1) + t // 2
                            if h == post_step(t) - 1:
                                wait(pool, s_ql[t % 2], 16 * (half + 1))
                                wait(pool, s_yn, b)
                                g = q_gate[:, t % 2, :].rearrange("p (h d) -> p h d", d=HD)
                                pool.tensor_tensor(g, g, y_now[:, t, :].unsqueeze(2).broadcast_to([P, H, HD]),
                                                   ALU.mult).then_inc(s_ym, 1)
                                wait(pool, s_qx, 16 * (n + 1))
                                wait(pool, s_ym, n + 1)
                                pool.tensor_tensor(q_gate[:, t % 2, :], q_gate[:, t % 2, :], q_xg[:, 0, :],
                                                   ALU.add).then_inc(s_yf, 1)
                            if h == min(post_step(t) + 4, H - 1):
                                wait(pool, s_x2, n + 1)
                                pool.tensor_tensor(q_h[:, t % 2, :], q_h[:, t % 2, :], x2[:, t % 2, :], ALU.add).then_inc(s_base, 1)
                    if ffn and h == 2:
                        wait(pool, s_ix, b - 1)
                        wait(pool, s_store[0], 128 * (b - 1))
                        wait(pool, s_store[1], 128 * (b - 1))
                        wait(pool, s_fo, b - 1)
                        wait(pool, s_sc, 16 * (b - 1))
                        plain(pool, b)
                        pool.indirect_dma_start(fx[:, :], None, xs_dram,
                                                bass.IndirectOffsetOnAxis(idx[:, 0:1], 0)).then_inc(s_fx, 16)
                        pool.tensor_copy(idx_out[:, :], idx[:, 1:2]).then_inc(s_ic, 1)
                        pool.tensor_copy(slot_w_now[:, :], slot_w[:, :]).then_inc(s_ic, 1)
                        pool.wait_ge(s_fx, 16 * (b - 1))
                if ffn:
                    wait(pool, s_fo, b)
                    plain(pool, b)
                    pool.indirect_dma_start(out, bass.IndirectOffsetOnAxis(idx_out[:, 0:1], 0), fx[:, :], None,
                                            compute_op=ALU.add)\
                        .then_inc(s_sc, 16)

            passes(pool, one)

        @block.scalar
        def _(act):
            act.preload_act_table_set(NATURAL_LOG_EXP)
            act.wait_ge(s_split, 1)

            def one(b, pre=False, ssm=False, before=False, post=False, ffn=False):
                if ssm:
                    wait(act, s_pe, TILES * (b + 1))
                    act.activation(db_raw[:, :], db_raw[:, :], ACT.Exp).then_inc(s_dbx, 1)
                    wait(act, s_dbx, b + 1)
                    wait(act, s_bc, H * b)
                    act.activation(edb[:, :], db_raw[:, :], ACT.Copy).then_inc(s_dbh, 1)
                    wait(act, s_u, H * b)
                    act.activation(eb[:, :], br_raw[:, :], ACT.Exp).then_inc(s_eb, 1)

                def decay(h):
                    i = H * b + h
                    wait(act, s_d, i + 1)
                    wait(act, s_scan, i - 1)
                    act.activation(a[:, h % ASLOTS, :], u[:, h % USLOTS, :], ACT.Exp, scale=a_t[:, h:h + 1]).then_inc(s_a, 1)

                for h in range(H):
                    if ssm:
                        wait(act, s_u, H * b + h + 1)
                        act.activation(u[:, h % USLOTS, :], u[:, h % USLOTS, :], ACT.Ln, bias=1.0).then_inc(s_d, 1)
                        if h:
                            decay(h - 1)
                        if h == 5:
                            wait(act, s_y, GROUPS * b)
                            act.activation(cc[:, :], c_raw[:, :], ACT.Copy).then_inc(s_cc, 1)
                    if pre:
                        for p in range(TILES // 2):
                            if h == 5 * p + 3:
                                n = 4 * (b + 1) + p
                                q = 2 * (p % 2)
                                wait(act, s_mv, 2 * n + 2)
                                act.activation(rstd[:, q:q + 2], mv[:, q:q + 2, 1], ACT.Ln, bias=eps_c).then_inc(s_ln, 1)
                                wait(act, s_ln, n + 1)
                                act.activation(rstd[:, q:q + 2], rstd[:, q:q + 2], ACT.Exp, scale=-0.5).then_inc(s_rs, 1)
                        for t in range(TILES):
                            n = TILES * (b + 1) + t
                            cols = slice(P * t, P * t + P)
                            if h == pre_step(t):
                                wait(act, s_pt, n + 1)
                                wait(act, s_pg, n)
                                act.activation(xt_hi[:, :, :].rearrange("p k n -> p (k n)"), ps_a[:, :], ACT.Copy).then_inc(s_xth, 1)
                            if h == pre_step(t) + 1:
                                wait(act, s_pp, n + 1)
                                if t == 0:
                                    wait(act, s_eb, b + 1)
                                    wait(act, s_edb, b + 1)
                                    wait(act, s_cc, b + 1)
                                act.activation(br_raw[:, cols], ps_a[:, 0:P], ACT.Copy)
                                act.activation(c_raw[:, cols], ps_a[:, P:2 * P], ACT.Copy)
                                act.activation(db_raw[:, cols], ps_a[0:2 * H, 2 * P:3 * P], ACT.Copy).then_inc(s_pe, 1)
                            if h == pre_step(t) + 2:
                                wait(act, s_pg, n + 1)
                                wait(act, s_spill[t % 2], 48 * (4 * (b + 1) + t // 2))
                                act.activation(gate[:, t % 2, :], ps_a[:, :], ACT.Exp, scale=-1.0).then_inc(s_ge, 1)
                            if h == pre_step(t) + 2:
                                wait(act, s_gm, n + 1)
                                act.activation(gate[:, t % 2, :], gate[:, t % 2, :], ACT.Ln, bias=1.0).then_inc(s_gl, 1)
                                wait(act, s_gl, n + 1)
                                act.activation(gate[:, t % 2, :], gate[:, t % 2, :], ACT.Exp, scale=-1.0).then_inc(s_gr, 1)
                    if post:
                        for t in range(TILES):
                            n = TILES * (b - 1) + t
                            if h == post_step(t):
                                wait(act, s_qt, n + 1)
                                wait(act, s_wo, n)
                                act.activation(yt_hi[:, :, :].rearrange("p k n -> p (k n)"), ps_b[:, :], ACT.Copy).then_inc(s_yth, 1)
                            if h == post_step(t) + 2:
                                wait(act, s_mv2, n + 1)
                                q = t % 2
                                act.activation(rstd2[:, q:q + 1], mv2[:, q, 1:2], ACT.Ln, bias=eps_c).then_inc(s_ln2, 1)
                                wait(act, s_ln2, n + 1)
                                act.activation(rstd2[:, q:q + 1], rstd2[:, q:q + 1], ACT.Exp, scale=-0.5).then_inc(s_rs2, 1)
                    if ffn:
                        if h == FFN_STEP:
                            wait(act, s_ft, b - 1)
                            act.activation(fxt[:, :, :].rearrange("p k n -> p (k n)"), ps_a[:, :], ACT.Copy).then_inc(s_fxt, 1)
                        if FFN_STEP < h <= FFN_STEP + 4:
                            j = h - FFN_STEP - 1
                            wait(act, s_ff, CHUNKS * (b - 2) + 2 * j + 2)
                            for f in range(4 * j, 4 * j + 4):
                                last = act.activation(hid[:, f, :], ps_a[:, P * (f % 4):P * (f % 4) + P], ACT.Identity,
                                                      bias=b1s[:, f:f + 1])
                            last.then_inc(s_hc, 1)
                        if h == FFN_STEP + 5:
                            wait(act, s_hc, 4 * (b - 1))
                            act.activation(hid[:, :, :], hid[:, :, :], ACT.Gelu).then_inc(s_gelu, 1)
                            act.preload_act_table_set(NATURAL_LOG_EXP)
                if ssm:
                    decay(H - 1)
                if post:
                    for half in range(2):
                        wait(act, s_lb, 2 * (b - 1) + half + 1)
                        act.activation(logit_row[:, 4 * half:4 * half + 4, :].rearrange("p k n -> p (k n)"), ps_b[:, :],
                                       ACT.Copy).then_inc(s_lr, 1)
                    wait(act, s_rmax, b)
                    act.activation(weigh[:, 0, :], logit[:, :], ACT.Exp, bias=small[:, 2:3]).then_inc(s_re, 1)

            passes(act, one)

        @block.tensor
        def _(pe):
            pe.wait_ge(s_setup, 2)
            pe.wait_ge(s_const, 16 * 9)
            pe.matmul(ps_b[0:TRAIN, :], one_hot[0:TRAIN, 0, 0:TRAIN], picked[0:TRAIN, 0:DM], start=True, stop=True)\
              .then_inc(s_tm, 1)
            pe.wait_ge(s_split, 1)

            def split_product(psum, lhs_hi, lhs_lo, rhs_hi, rhs_lo, more=False):
                parts = [(lhs_hi, rhs_hi), (lhs_lo, rhs_hi), (lhs_hi, rhs_lo)]
                for k in range(KC):
                    for j, (lhs, rhs) in enumerate(parts):
                        last = pe.matmul(psum, lhs[:, k, :], rhs[:, k, :], start=(k == 0 and j == 0),
                                         stop=(k == KC - 1 and j == 2 and not more))
                return last

            def one(b, pre=False, ssm=False, before=False, post=False, ffn=False):
                def broadcast(h):
                    i = H * b + h
                    if h == 0:
                        wait(pe, s_edb, b + 1)
                    wait(pe, s_u, i - 1)
                    for half in range(2):
                        last = pe.matmul(ps_e[:, h % 2, 512 * half:512 * half + 512],
                                         head_sel[:, h:h + 1].broadcast_to([2 * H, P]),
                                         edb[:, 512 * half:512 * half + 512], start=True, stop=True)
                    last.then_inc(s_bc, 1)

                def contract(c, g, half):
                    if half == 0:
                        wait(pe, s_scan, H * c + GROUP * (g + 1))
                        wait(pe, s_pick, GROUPS * c + g)
                        if g == 0:
                            wait(pe, s_cc, c + 1)
                    for k in range(16 * half, 16 * half + 16):
                        q, j = k % 4, k // 4
                        last = pe.matmul(ps_y[BLK * q:BLK * q + BLK, P * j:P * j + P],
                                         cc[:, BLK * k:BLK * k + BLK],
                                         x[:, g % 2, :, BLK * k:BLK * k + BLK], start=True, stop=True,
                                         tile_position=(0, BLK * q))
                    if half:
                        last.then_inc(s_y, 1)

                if ssm:
                    broadcast(0)
                for h in range(H):
                    g, left = h // GROUP - 1, h % GROUP
                    if left >= 2 and (ssm if g >= 0 else before):
                        contract(b if g >= 0 else b - 1, g % GROUPS, left - 2)
                    if pre:
                        for t in range(TILES):
                            n = TILES * (b + 1) + t
                            if h == pre_step(t):
                                wait(pe, s_xn, n + 1)
                                wait(pe, s_ge, n)
                                if t == 0:
                                    wait(pe, s_ol, b - 1)
                                for k in range(KC):
                                    last = pe.transpose(ps_a[:, P * k:P * k + P], xn[:, t % 2, P * k:P * k + P], ident[:, :])
                                last.then_inc(s_pt, 1)
                    if ssm and h + 1 < H:
                        broadcast(h + 1)
                    if pre:
                        for t in range(TILES):
                            n = TILES * (b + 1) + t
                            if h == pre_step(t):
                                wait(pe, s_xtl, n + 1)
                                split_product(ps_a[:, 0:P], wx_hi[:, :, 0:N], wx_lo[:, :, 0:N], xt_hi, xt_lo)
                                split_product(ps_a[:, P:2 * P], wx_hi[:, :, N:2 * N], wx_lo[:, :, N:2 * N], xt_hi, xt_lo)
                                split_product(ps_a[0:2 * H, 2 * P:3 * P], wx_hi[:, :, 2 * N:PROJ], wx_lo[:, :, 2 * N:PROJ],
                                              xt_hi, xt_lo).then_inc(s_pp, 1)
                            if h == pre_step(t) + 1:
                                wait(pe, s_pe, n + 1)
                                split_product(ps_a[:, :], xt_hi, xt_lo, wg_hi, wg_lo, more=True)
                                pe.matmul(ps_a[:, :], ones_r[:, :], bias_g[:, :], start=False, stop=True).then_inc(s_pg, 1)
                    if post:
                        for t in range(TILES):
                            n = TILES * (b - 1) + t
                            if h == post_step(t):
                                wait(pe, s_yf, n + 1)
                                wait(pe, s_h1, n)
                                if t == 0:
                                    wait(pe, s_ix, b - 1)
                                for k in range(KC):
                                    last = pe.transpose(ps_b[:, P * k:P * k + P], q_gate[:, t % 2, P * k:P * k + P], ident[:, :])
                                last.then_inc(s_qt, 1)
                            if h == post_step(t) + 1:
                                wait(pe, s_ytl, n + 1)
                                split_product(ps_b[:, :], yt_hi, yt_lo, wo_hi, wo_lo).then_inc(s_wo, 1)
                    if ffn:
                        if h == FFN_STEP:
                            wait(pe, s_fx, 16 * (b - 1))
                            if pre:
                                wait(pe, s_ge, TILES * (b + 2))
                            for k in range(KC):
                                last = pe.transpose(ps_a[:, P * k:P * k + P], fx[:, P * k:P * k + P], ident[:, :])
                            last.then_inc(s_ft, 1)
                        if FFN_STEP < h <= FFN_STEP + 4:
                            j = h - FFN_STEP - 1
                            if j == 0:
                                wait(pe, s_fxt, b - 1)
                            else:
                                wait(pe, s_hc, 4 * (b - 2) + j)
                            for c in (2 * j, 2 * j + 1):
                                wait(pe, s_w[c % 2], 16 * (HALF * (b - 2) + c // 2 + 1))
                                w = ffn_w[:, c % 2, :].rearrange("p (k n) -> p k n", k=KC)
                                for f in range(2):
                                    col = P * (2 * (c % 2) + f)
                                    for k in range(KC):
                                        last = pe.matmul(ps_a[:, col:col + P], w[:, k, P * f:P * f + P], fxt[:, k, :],
                                                         start=(k == 0), stop=(k == KC - 1))
                                last.then_inc(s_ff, 1)
                if post:
                    wait(pe, s_dg, b)
                    wait(pe, s_h1, TILES * b)
                    for half in range(2):
                        if half:
                            wait(pe, s_lr, 2 * (b - 1) + 1)
                        pe.matmul(ps_b[:, :], ones[:, :], one_hot[:, 4 * half:4 * half + 4, :], start=True, stop=True)\
                          .then_inc(s_lb, 1)
                if ffn:
                    wait(pe, s_gelu, b - 1)
                    for c in range(HALF, CHUNKS):
                        wait(pe, s_w[c % 2], 16 * (HALF * (b - 2) + c // 2 + 1))
                        w = ffn_w[:, c % 2, :].rearrange("p (f n) -> p f n", f=2)
                        for j in range(2):
                            f = 2 * (c - HALF) + j
                            last = pe.matmul(ps_a[:, :], hid[:, f, :], w[:, j, :], start=(f == 0), stop=(f == FT - 1))
                        last.then_inc(s_ff, 1)
                if post:
                    wait(pe, s_es, b)
                    wait(pe, s_lr, 2 * b)
                    pe.matmul(ps_b[:, 0:1], ones[:, :], weigh[:, 3, 0:1], start=True, stop=True).then_inc(s_z, 1)
                    wait(pe, s_rv, b)
                    wait(pe, s_oh, b)
                    for t in range(TILES):
                        last = pe.matmul(ps_b[:, 2:6], one_hot[:, t, :], slot_rhs[:, t, :], start=(t == 0), stop=(t == TILES - 1))
                    last.then_inc(s_sl, 1)

            passes(pe, one)

        @block.vector
        def _(dve):
            n_link = [0]

            def link(ins):
                n_link[0] += 1
                ins.then_inc(s_r, 1)
                dve.wait_ge(s_r, n_link[0])

            dve.memset(eps_c, EPS)
            link(dve.memset(small[:, 4:5], 0.0))
            dve.wait_ge(s_ids, 48)
            tr_f, tc_f, wrap = rank[:, :, :].rearrange("p a b -> p (a b)"), small[0:TRAIN, 8:9], small[0:TRAIN, 9:10]
            wrap_ids = y_next[:, 0:2, :].rearrange("p a b -> p (a b)")
            for src, dst, tmp in ((id_i[:, :], id_f[:, :], wrap_ids), (row_i[:, :], tr_f, wrap_ids),
                                  (id_now[0:TRAIN, 0:1], tc_f, wrap)):
                link(dve.tensor_copy(dst, src))
                link(dve.tensor_scalar(tmp, dst, 0.0, float(VOCAB), ALU.is_lt, ALU.mult))
                link(dve.tensor_tensor(dst, dst, tmp, ALU.add))
            link(dve.tensor_scalar(id_f[:, :], id_f[:, :], 0.0, float(VOCAB - 1), ALU.max, ALU.min))
            link(dve.tensor_copy(id_i[:, :], id_f[:, :]))
            link(dve.tensor_scalar(wrap, tc_f, 0.0, float(VOCAB - 1), ALU.max, ALU.min))
            dve.tensor_copy(id_now[0:TRAIN, 0:1], wrap).then_inc(s_setup, 1)
            dve.wait_ge(s_iota, 4)
            dve.tensor_scalar(one_hot[0:TRAIN, 0, 0:TRAIN], tr_f[0:TRAIN, :], tc_f, None, ALU.is_equal).then_inc(s_setup, 1)
            eq = x[:, 0, :, :].rearrange("p a b -> p (a b)").rearrange("p (t j) -> p t j", j=TRAIN)
            dve.wait_ge(s_wload, 64)
            dve.wait_ge(s_const, 144)
            stage = x[:, 0, :, :].rearrange("p a b -> p (a b)")[:, 0:KC * PROJ].rearrange("p (k n) -> p k n", k=KC)
            wg_st = x[:, 1, 0:2, :].rearrange("p a (b n) -> p (a b) n", n=DM)
            wo_st = x[:, 1, 2:4, :].rearrange("p a (b n) -> p (a b) n", n=DM)
            dve.tensor_copy(wx_hi[:, :, :], stage)
            dve.tensor_copy(wg_hi[:, :, :], wg_st)
            link(dve.tensor_copy(wo_hi[:, :, :], wo_st))
            dve.tensor_tensor(wx_lo[:, :, :], stage, wx_hi[:, :, :].bitcast(F32), ALU.subtract)
            dve.tensor_tensor(wg_lo[:, :, :], wg_st, wg_hi[:, :, :].bitcast(F32), ALU.subtract)
            link(dve.tensor_tensor(wo_lo[:, :, :], wo_st, wo_hi[:, :, :].bitcast(F32), ALU.subtract))
            link(dve.tensor_tensor(eq, id_f[:, :].unsqueeze(2).broadcast_to([P, B * TILES, TRAIN]),
                                   tr_f.unsqueeze(1).broadcast_to([P, B * TILES, TRAIN]), ALU.is_equal))
            link(dve.tensor_scalar(wrap_ids, slot_iota[:, 0:TRAIN], -1.0, float(TRAIN), ALU.mult, ALU.add))
            link(dve.tensor_tensor(eq, eq, wrap_ids.unsqueeze(1).broadcast_to([P, B * TILES, TRAIN]), ALU.mult))
            link(dve.tensor_reduce(id_f[:, :], eq, axis=AX.X, op=ALU.max))
            link(dve.tensor_scalar(id_f[:, :], id_f[:, :], -1.0, float(TRAIN), ALU.mult, ALU.add))
            dve.tensor_copy(row_i[:, :], id_f[:, :]).then_inc(s_setup, 1)
            dve.wait_ge(s_sc, 16)
            dve.wait_ge(s_tm, 1)
            dve.tensor_tensor(picked[0:TRAIN, DM:2 * DM], u[0:TRAIN, 3, 0:DM], ps_b[0:TRAIN, :], ALU.add).then_inc(s_stage, 1)
            dve.sem_inc(s_fo, 1)
            dve.sem_inc(s_ol, 1)
            link(dve.tensor_reduce(diag32[:, :], ident[:, :].rearrange("p (g c) -> p c g", c=BLK), axis=AX.X, op=ALU.add))
            link(dve.tensor_copy(head_sel[:, :], diag32[0:2 * H, :]))
            link(dve.tensor_copy(ones_r[:, :], ones[0:2 * BLK, :]))
            link(dve.tensor_copy(x2[:, 0, 0:H], dp_row[:, 0:H]))
            link(dve.tensor_copy(dp_row[:, :].rearrange("p (h d) -> p h d", d=HD),
                                 x2[:, 0, 0:H].unsqueeze(2).broadcast_to([P, H, HD])))
            link(dve.memset(slot_rhs[:, :, 3], 0.0))
            link(dve.tensor_copy(slot_rhs[:, :, 0], token_no[:, :]))
            link(dve.memset(x2[0:2 * BLK, 1, :], 0.0))
            link(dve.tensor_copy(bias_g[:, :], x2[0:2 * BLK, 1, :]))
            link(dve.tensor_copy(bias_g[0:1, :], q_gate[0:1, 0, :]))
            link(dve.tensor_copy(bias_g[BLK:BLK + 1, :], q_gate[BLK:BLK + 1, 0, :]))
            link(dve.tensor_tensor(x2[BLK:BLK + 1, 0, :], q_gate[BLK:BLK + 1, 0, :], bias_g[BLK:BLK + 1, :].bitcast(F32), ALU.subtract))
            link(dve.tensor_copy(bias_g[BLK:BLK + 1, :], x2[BLK:BLK + 1, 0, :]))
            dve.memset(small[:, 4:5], 0.0).then_inc(s_split, 1)

            links = n_link[0]
            RL = 8 + 4 * TILES

            def router(b):
                count = [0]

                def chain(ins):
                    count[0] += 1
                    ins.then_inc(s_r, 1)

                def chained():
                    dve.wait_ge(s_r, links + RL_TOTAL * b + count[0])

                dve.wait_ge(s_lg, TILES * (b + 1))
                wait(dve, s_sl, b)
                dve.tensor_tensor(one_hot[:, :, :], ident[:, :].unsqueeze(1).broadcast_to([P, TILES, P]),
                                  logit[:, :].unsqueeze(2).broadcast_to([P, TILES, P]), ALU.mult).then_inc(s_dg, 1)
                dve.wait_ge(s_lr, 2 * b + 2)
                flat = logit_row.rearrange("p k n -> p (k n)")
                chain(dve.tensor_reduce(small[:, 3:4], flat, axis=AX.X, op=ALU.max))
                for q in range(4):
                    if q in (0, 3):
                        chain(dve.memset(rank[:, q, :], 0.0))
                chained()
                dve.tensor_scalar(small[:, 2:3], small[:, 3:4], -1.0, None, ALU.mult).then_inc(s_rmax, 1)
                junk = one_hot[:, :, :].rearrange("p t c -> p (t c)")
                for t in range(TILES):
                    mine = logit[:, t:t + 1]
                    row = lambda lo, hi: flat[:, P * lo:P * hi]
                    chained()
                    if t:
                        chain(dve.tensor_scalar(junk[:, 0:P * t], row(0, t), mine, 0.0, ALU.is_ge, ALU.add,
                                                accum_out=rank[:, 0, t:t + 1]))
                    if t:
                        chained()
                    chain(dve.tensor_scalar(junk[:, 0:P * (TILES - t)], row(t, TILES), mine, 0.0, ALU.is_gt, ALU.add,
                                            accum_out=rank[:, 1, t:t + 1]))
                    chained()
                    chain(dve.scalar_tensor_tensor(junk[:, 0:P], row(t, t + 1), mine, before[:, :], ALU.is_equal, ALU.mult,
                                                   accum_out=rank[:, 2, t:t + 1]))
                chained()
                chain(dve.tensor_tensor(rank[:, 4, :], rank[:, 0, :], rank[:, 1, :], ALU.add))
                chained()
                chain(dve.tensor_tensor(rank[:, 5, :], rank[:, 4, :], rank[:, 2, :], ALU.add))
                chained()
                chain(dve.tensor_scalar(weigh[:, 1, :], rank[:, 5, :], float(KEEP), None, ALU.is_lt))
                dve.wait_ge(s_re, b + 1)
                chained()
                chain(dve.tensor_tensor(weigh[:, 2, :], weigh[:, 0, :], weigh[:, 1, :], ALU.mult))
                chained()
                dve.tensor_reduce(weigh[:, 3, 0:1], weigh[:, 2, :], axis=AX.X, op=ALU.add).then_inc(s_es, 1)
                for t in range(TILES):
                    last = dve.tensor_scalar(one_hot[:, t, :], slot_iota[:, :], rank[:, 5, t:t + 1], None, ALU.is_equal)
                last.then_inc(s_oh, 1)
                chain(dve.tensor_copy(slot_rhs[:, :, 1], token_no[:, :]))
                dve.wait_ge(s_z, b + 1)
                chain(dve.reciprocal(small[:, 5:6], ps_b[:, 0:1]))
                chained()
                dve.tensor_scalar(slot_rhs[:, :, 2], weigh[:, 2, :], small[:, 5:6], None, ALU.mult).then_inc(s_rv, 1)
                chain(dve.tensor_scalar(token_no[:, :], token_no[:, :], float(L), None, ALU.add))
                dve.wait_ge(s_sl, b + 1)
                wait(dve, s_ic, 2 * b)
                wait(dve, s_fx, 16 * b)
                chain(dve.tensor_copy(slot_w[:, :], ps_b[:, 4:5]))
                dve.tensor_copy(idx[:, :], ps_b[:, 2:4]).then_inc(s_ix, 1)
                return count[0]

            RL_TOTAL = 3 + (TILES - 1) + 2 * TILES + 4 + 4

            def one(b, pre=False, ssm=False, before=False, post=False, ffn=False):
                if ssm:
                    wait(dve, s_dbh, b + 1)
                    dve.tensor_tensor(edb[H:2 * H, :], db_raw[H:2 * H, :], edb[H:2 * H, :].bitcast(F32), ALU.subtract)\
                       .then_inc(s_edb, 1)

                def scan(c, h):
                    i = H * c + h
                    s = x[:, h // GROUP % 2, h % GROUP, :]
                    wait(dve, s_a, i + 1)
                    wait(dve, s_x, i + 1)
                    dve.tensor_tensor_scan(s, a[:, h % ASLOTS, :], s, 0.0, ALU.mult, ALU.add).then_inc(s_scan, 1)

                def pick(c, g):
                    n = GROUPS * c + g
                    wait(dve, s_y, n + 1)
                    wait(dve, s_yr, n)
                    v = "p (b c) -> p b c"
                    dve.tensor_tensor(picked[:, :].rearrange(v, c=BLK), ps_y[:, :].rearrange(v, c=BLK),
                                      diag32[:, :].unsqueeze(1).broadcast_to([P, TILES * GROUP, BLK]), ALU.mult).then_inc(s_pick, 1)
                    wait(dve, s_pick, n + 1)
                    if g == 0:
                        wait(dve, s_yn, c)
                    dve.tensor_reduce(y_next[:, :, GROUP * g:GROUP * g + GROUP],
                                      picked[:, :].rearrange("p (t h c) -> p t h c", h=GROUP, c=BLK), axis=AX.X, op=ALU.add)\
                       .then_inc(s_yr, 1)

                for h in range(H):
                    if ssm:
                        i = H * b + h
                        if h == 0:
                            wait(dve, s_eb, b + 1)
                        wait(dve, s_bc, i + 1)
                        wait(dve, s_a, i - USLOTS + 1)
                        wait(dve, s_x, i - USLOTS + 1)
                        dve.tensor_tensor(u[:, h % USLOTS, :], ps_e[:, h % 2, :], eb[:, :], ALU.mult).then_inc(s_u, 1)
                    if h >= 2 and ssm:
                        scan(b, h - 2)
                    if h < 2 and before:
                        scan(b - 1, H - 2 + h)
                    g = h // GROUP - 2
                    if h % GROUP == 0 and (ssm if g >= 0 else before):
                        pick(b if g >= 0 else b - 1, g % GROUPS)
                    if pre:
                        for p in range(TILES // 2):
                            n = 4 * (b + 1) + p
                            if h == 5 * p + 3:
                                wait(dve, s_g2[p % 2], 32 * (2 * (b + 1) + p // 2 + 1))
                                for j in range(2):
                                    dve.bn_stats(stats[:, (2 * p + j) % 4, :], emb[:, (2 * p + j) % 4, :]).then_inc(s_st, 1)
                                for j in range(2):
                                    wait(dve, s_st, 2 * n + j + 1)
                                    plain(dve, b)
                                    dve.bn_aggr(mv[:, (2 * p + j) % 4, :], stats[:, (2 * p + j) % 4, :]).then_inc(s_mv, 1)
                        for t in range(TILES):
                            n = TILES * (b + 1) + t
                            if h == pre_step(t) - 1 + (t % 2):
                                wait(dve, s_rs, 4 * (b + 1) + t // 2 + 1)
                                wait(dve, s_spill[t % 2], 48 * (4 * (b + 1) + t // 2))
                                dve.tensor_scalar(xn[:, t % 2, :], emb[:, t % 4, :], mv[:, t % 4, 0:1], rstd[:, t % 4:t % 4 + 1],
                                                  ALU.subtract, ALU.mult).then_inc(s_xn, 1)
                            if h == pre_step(t):
                                wait(dve, s_xth, n + 1)
                                dve.tensor_tensor(xt_lo[:, :, :].rearrange("p k n -> p (k n)"), ps_a[:, :],
                                                  xt_hi[:, :, :].rearrange("p k n -> p (k n)").bitcast(F32), ALU.subtract).then_inc(s_xtl, 1)
                            if h == pre_step(t) + 2:
                                wait(dve, s_ge, n + 1)
                                dve.tensor_scalar(gate[:, t % 2, :], gate[:, t % 2, :], BIG, None, ALU.min).then_inc(s_gm, 1)
                    if post:
                        for t in range(TILES):
                            n = TILES * (b - 1) + t
                            q = t % 2
                            if h == post_step(t):
                                wait(dve, s_yth, n + 1)
                                dve.tensor_tensor(yt_lo[:, :, :].rearrange("p k n -> p (k n)"), ps_b[:, :],
                                                  yt_hi[:, :, :].rearrange("p k n -> p (k n)").bitcast(F32), ALU.subtract).then_inc(s_ytl, 1)
                            if h == post_step(t) + 2:
                                wait(dve, s_wo, n + 1)
                                wait(dve, s_qh[q], 16 * (4 * (b - 1) + t // 2 + 1))
                                dve.tensor_tensor(q_h[:, q, :], q_h[:, q, :], ps_b[:, :], ALU.add).then_inc(s_h1, 1)
                                wait(dve, s_h1, n + 1)
                                dve.bn_stats(stats2[:, q, :], q_h[:, q, :]).then_inc(s_st2, 1)
                                wait(dve, s_st2, n + 1)
                                plain(dve, b)
                                dve.bn_aggr(mv2[:, q, :], stats2[:, q, :]).then_inc(s_mv2, 1)
                            if h == min(post_step(t) + 3, H - 1):
                                wait(dve, s_rs2, n + 1)
                                wait(dve, s_store[q], 32 * (4 * (b - 1) + t // 2))
                                wait(dve, s_base, n - 1)
                                dve.tensor_scalar(x2[:, q, :], q_h[:, q, :], mv2[:, q, 0:1], rstd2[:, q:q + 1],
                                                  ALU.subtract, ALU.mult).then_inc(s_x2, 1)
                                wait(dve, s_x2, n + 1)
                                if t == 0:
                                    wait(dve, s_re, b - 1)
                                    wait(dve, s_dg, b - 1)
                                    wait(dve, s_sl, b - 1)
                                wait(dve, s_lg, n)
                                dve.tensor_tensor_reduce(out=one_hot[:, 0:4, :].rearrange("p t c -> p (t c)"), in0=x2[:, q, :], in1=wr_row[:, :], scale=1.0,
                                                         scalar=br_c, op0=ALU.mult, op1=ALU.add,
                                                         accum_out=logit[:, t:t + 1]).then_inc(s_lg, 1)
                if post:
                    assert router(b - 1) == RL_TOTAL, router
                if ffn:
                    wait(dve, s_ff, CHUNKS * (b - 1))
                    wait(dve, s_ic, 2 * (b - 1))
                    dve.tensor_tensor(fx[:, :], ps_a[:, :], b2_row[:, :], ALU.add).then_inc(s_ol, 1)
                    wait(dve, s_ol, b)
                    dve.tensor_scalar(fx[:, :], fx[:, :], slot_w_now[:, 0:1], None, ALU.mult).then_inc(s_fo, 1)

            passes(dve, one)


def kernel(**inputs):
    import numpy as np
    import concourse.bacc as bacc
    from concourse.bass_utils import run_bass_kernel_spmd

    g = {k: np.asarray(v) for k, v in inputs.items()}
    flat = lambda v: np.ascontiguousarray(v.reshape(1, -1))
    arrays = {
        "ids": np.ascontiguousarray(g["x"].reshape(B * TILES, P).T),
        "W": np.ascontiguousarray(g["L0_tok_W"]),
        "delta_t": np.ascontiguousarray(g["L0_tok_delta"].reshape(DM, TRAIN).T),
        "train_row": flat(g["L0_tok_token_indices"]),
        "train_col": np.ascontiguousarray(g["L0_tok_token_indices"].reshape(-1, 1)),
        "Wx": np.ascontiguousarray(g["L0_attn_Wx"]),
        "Wg": np.ascontiguousarray(g["L0_attn_Wg"]),
        "bg": flat(g["L0_attn_bg"]),
        "Wo": np.ascontiguousarray(g["L0_attn_Wo"]),
        "A_t": np.ascontiguousarray(g["L0_attn_A"].T),
        "Dp": flat(g["L0_attn_Dp"]),
        "Wr": flat(g["L0_ffn_Wr"]),
        "br": flat(g["L0_ffn_br"]),
        "W1": np.ascontiguousarray(g["L0_ffn_W1"]),
        "b1_t": np.ascontiguousarray(g["L0_ffn_b1"].reshape(FT, P).T),
        "W2": np.ascontiguousarray(g["L0_ffn_W2"]),
        "b2": flat(g["L0_ffn_b2"]),
    }
    nc = bacc.Bacc("TRN2", target_bir_lowering=False, num_devices=1)
    aps = {k: nc.dram_tensor(k, v.shape, mybir.dt.from_np(v.dtype), kind="ExternalInput").ap() for k, v in arrays.items()}
    out = nc.dram_tensor("out", [B * L, DM], F32, kind="ExternalOutput").ap()
    build(nc, out=out, **aps)
    r = run_bass_kernel_spmd(nc, [arrays], core_ids=[0])
    return r.results[0]["out"].reshape(B, L, DM)
```

```python
import concourse.bass as bass
from concourse import mybir
from contextlib import ExitStack

F32 = mybir.dt.float32
F32R = mybir.dt.float32r
I32 = mybir.dt.int32
ALU = mybir.AluOpType
ACT = mybir.ActivationFunctionType
AX = mybir.AxisListType

P = 128
B, L, DM = 8, 1024, 512
H, N = 32, 128
HD = DM // H
VOCAB, TRAIN = 32000, 64
DFF = 4 * DM
KEEP = L // 8
KC = DM // P
TILES = L // P
FT = DFF // P
PROJ = 2 * N + 2 * H
EPS = 1e-5
BIG = float(2 ** 62)
SAFE = 22.0
GROUP = 4
GROUPS = H // GROUP
BLK = 32
USLOTS, ASLOTS, RING = 4, 2, 3
CHUNKS = 16
HALF = CHUNKS // 2
NATURAL_LOG_EXP = "natural_log_exp_and_others"

def pre_step(t):
    return 4 + 3 * t

def gather_step(p):
    return max(6 * p - 2, 0)

def post_step(t):
    return 6 + 3 * t

FLAG_STEP = 29

WO_STEP = 6

FX_STEP = 7

def chunk_step(c):
    return FX_STEP + 2 + (c if c < HALF else c + 1)


def build(nc, ids, W, delta_t, train_row, train_col, Wx, Wg, bg, Wo, A_t, Dp, Wr, br, W1, b1_t, W2, b2, out):
    xs_dram = nc.dram_tensor("normed2", [L, DM], F32, kind="Internal").ap()
    gate_dram = nc.dram_tensor("gates", [B * L, DM], F32, kind="Internal").ap()
    xd_dram = nc.dram_tensor("skip", [B * L, DM], F32, kind="Internal").ap()
    h0_dram = nc.dram_tensor("embedded", [B * L, DM], F32, kind="Internal").ap()
    adapted_dram = nc.dram_tensor("adapted", [TRAIN, DM], F32, kind="Internal").ap()

    ctx = ExitStack()
    with ctx:
        def sb(name, shape, dt=F32):
            return ctx.enter_context(nc.sbuf_tensor(name, shape, dt))

        def sem(name):
            return ctx.enter_context(nc.semaphore(name))

        ident = sb("ident", [P, P])
        slot_iota = sb("slot_iota", [P, P])
        before = sb("before", [P, P])
        ones = sb("ones", [P, P])
        ones_r = sb("ones_r", [2 * BLK, P], F32R)
        diag32 = sb("diag32", [P, BLK])
        head_sel = sb("head_sel", [2 * H, H], F32R)
        dp_row = sb("dp_row", [P, DM])
        wr_row = sb("wr_row", [P, DM])
        b2_row = sb("b2_row", [P, DM])
        bias_g = sb("bias_g", [2 * BLK, DM], F32R)
        a_t = sb("a_t", [N, H])
        b1s = sb("b1s", [P, FT])
        small = sb("small", [P, 48])
        eps_c, br_c = small[:, 0:1], small[:, 1:2]
        wx_hi, wx_lo = sb("wx_hi", [P, KC, PROJ], F32R), sb("wx_lo", [P, KC, PROJ], F32R)
        wg_hi, wg_lo = sb("wg_hi", [P, KC, DM], F32R), sb("wg_lo", [P, KC, DM], F32R)
        wo_hi, wo_lo = sb("wo_hi", [P, KC, DM], F32R), sb("wo_lo", [P, KC, DM], F32R)
        ffn_w = sb("ffn_w", [P, 2, 1024])
        id_f, id_i = sb("id_f", [P, B * TILES]), sb("id_i", [P, B * TILES], I32)
        row_i = sb("row_i", [P, B * TILES], I32)
        id_now, row_now = sb("id_now", [P, TILES], I32), sb("row_now", [P, TILES], I32)
        token_no = sb("token_no", [P, TILES])
        br_raw, c_raw, db_raw = sb("b_raw", [N, L]), sb("c_raw", [N, L]), sb("db_raw", [2 * H, L])
        eb, cc, edb = sb("exp_b", [N, L]), sb("c_now", [N, L]), sb("exp_db", [2 * H, L], F32R)
        u = sb("u", [N, USLOTS, L])
        a = sb("decay", [N, ASLOTS, L])
        x = sb("states", [N, 2, GROUP, L])
        picked = sb("picked", [P, DM])
        y_next, y_now = sb("y_next", [P, TILES, H]), sb("y_now", [P, TILES, H])
        emb = sb("emb", [P, 4, DM])
        xn = sb("xn", [P, 2, DM])
        xt_hi, xt_lo = sb("xt_hi", [P, KC, P], F32R), sb("xt_lo", [P, KC, P], F32R)
        proj = sb("proj", [P, PROJ])
        gate = sb("gate", [P, 2, DM])
        stats, mv, rstd = sb("stats", [P, 4, 6]), sb("mv", [P, 4, 2]), sb("rstd", [P, 4])
        q_gate, q_xd, q_h = sb("q_gate", [P, 2, DM]), sb("q_xd", [P, 1, DM]), sb("q_h", [P, 2, DM])
        yt_hi, yt_lo = sb("yt_hi", [P, KC, P], F32R), sb("yt_lo", [P, KC, P], F32R)
        x2 = sb("x2", [P, 2, DM])
        stats2, mv2, rstd2 = sb("stats2", [P, 2, 6]), sb("mv2", [P, 2, 2]), sb("rstd2", [P, 2])
        logit = sb("logit", [P, TILES])
        rank = sb("rank", [P, 8, TILES])
        weigh = sb("weigh", [P, 4, TILES])
        slot_rhs = sb("slot_rhs", [P, TILES, 4])
        idx, idx_out = sb("idx", [P, 2], I32), sb("idx_out", [P, 1], I32)
        unsafe = sb("unsafe", [P, 4])
        careful_i = sb("careful_i", [1, 1], I32)
        slot_w, slot_w_now = sb("slot_w", [P, 1]), sb("slot_w_now", [P, 1])
        fx, fxt = sb("fx", [P, DM]), sb("fxt", [P, KC, P])
        hid = sb("hid", [P, FT, P])
        one_hot = sb("one_hot", [P, TILES, P])
        logit_row = sb("logit_row", [P, TILES, P])
        deltas = logit_row[0:TRAIN, 0:KC, :].rearrange("p k n -> p (k n)")
        adapted = logit_row[0:TRAIN, KC:TILES, :].rearrange("p k n -> p (k n)")

        ps_e = ctx.enter_context(nc.psum_tensor("ps_e", [P, RING, DM], F32))
        ps_y = ctx.enter_context(nc.psum_tensor("ps_y", [P, DM], F32))
        ps_t = ctx.enter_context(nc.psum_tensor("ps_t", [P, DM], F32))
        ps_p = ctx.enter_context(nc.psum_tensor("ps_p", [P, DM], F32))
        ps_b = ctx.enter_context(nc.psum_tensor("ps_b", [P, DM], F32))
        ps_f = ctx.enter_context(nc.psum_tensor("ps_f", [P, DM], F32))

        s_passed = {nc.sync.engine: sem("sp_passed"), nc.gpsimd.engine: sem("pool_passed"), nc.vector.engine: sem("dve_passed"),
                    nc.scalar.engine: sem("act_passed")}
        s_const, s_ids, s_stage, s_wload = sem("const_loaded"), sem("ids_loaded"), sem("table_built"), sem("weights_loaded")
        s_iota, s_zero, s_setup, s_split, s_wsplit = (
            sem("iota_done"), sem("zero_done"), sem("setup_done"), sem("split_done"), sem("wo_split"))
        s_tm, s_ta = sem("table_mm"), sem("table_stored")
        s_eb, s_cc, s_dbx, s_dbh, s_edb = sem("eb_ready"), sem("cc_ready"), sem("db_exp"), sem("db_hi"), sem("edb_ready")
        s_bc, s_u, s_d, s_a, s_x = sem("bcast_done"), sem("u_ready"), sem("d_ready"), sem("a_ready"), sem("x_ready")
        s_scan, s_y, s_pick, s_yr, s_yn = sem("scan_done"), sem("contracted"), sem("picked_ready"), sem("y_ready"), sem("y_now_ready")
        s_idn = sem("ids_now")
        s_g1, s_g2 = [sem("rows_even"), sem("rows_odd")], [sem("adapted_even"), sem("adapted_odd")]
        s_st, s_mv, s_ln, s_rs, s_xn = sem("stats_ready"), sem("mv_ready"), sem("lnv_ready"), sem("rstd_ready"), sem("xn_ready")
        s_pt, s_xth, s_xtl, s_pp, s_pe = sem("pre_t"), sem("xt_hi_ready"), sem("xt_lo_ready"), sem("pre_proj"), sem("pre_evac")
        s_pg, s_ge, s_gm, s_gl, s_gr = sem("gate_mm"), sem("gate_exp"), sem("gate_min"), sem("gate_ln"), sem("gate_ready")
        s_mx, s_ind, s_cnt, s_tot, s_flag = sem("max_ready"), sem("unsafe_ready"), sem("unsafe_count"), sem("unsafe_total"), sem("flag_ready")
        s_abs, s_l1, s_sp = sem("abs_ready"), sem("log_part_ready"), sem("softplus_ready")
        s_pj, s_pb = sem("proj_copied"), sem("proj_t")
        s_xd = sem("skip_ready")
        s_hs = [sem("rows_spilled_even"), sem("rows_spilled_odd")]
        s_xs = [sem("skip_spilled_even"), sem("skip_spilled_odd")]
        s_gs = [sem("gate_spilled_even"), sem("gate_spilled_odd")]
        s_qh = [sem("post_h_even"), sem("post_h_odd")]
        s_ql, s_qx = [sem("post_load_even"), sem("post_load_odd")], sem("post_load_xg")
        s_ym, s_yf, s_qt, s_yth, s_ytl = sem("y_gated"), sem("y_full"), sem("post_t"), sem("yt_hi_ready"), sem("yt_lo_ready")
        s_wo, s_h1, s_st2, s_mv2, s_ln2, s_rs2 = sem("wo_done"), sem("h1_ready"), sem("stats2_ready"), sem("mv2_ready"), sem("lnv2_ready"), sem("rstd2_ready")
        s_x2, s_lg, s_base = sem("x2_ready"), sem("logit_ready"), sem("base_ready")
        s_store = [sem("store_even"), sem("store_odd")]
        s_dg, s_lb, s_lr = sem("diag_ready"), sem("logit_bcast"), sem("logit_row_ready")
        s_r, s_rmax, s_re, s_es, s_z, s_rv, s_oh, s_sl, s_ix, s_sw = (
            sem("rank_chain"), sem("row_max"), sem("row_exp"), sem("exp_sum"), sem("z_done"), sem("slot_rhs_ready"),
            sem("one_hot_ready"), sem("slots_done"), sem("idx_ready"), sem("slot_w_ready"))
        s_fx,  s_ic, s_ft, s_fxt = sem("fx_loaded"), sem("idx_copied"), sem("fx_t"), sem("fxt_ready")
        s_w = [sem("chunk_even"), sem("chunk_odd")]
        s_ff, s_hc, s_gelu, s_ol, s_fo, s_sc = sem("chunk_used"), sem("hid_copied"), sem("gelu_done"), sem("ffn_sum"), sem("ffn_out"), sem("scattered")

        block = ctx.enter_context(nc.Block())

        def wait(eng, s, value):
            if not isinstance(value, int) or value > 0:
                eng.wait_ge(s, value)

        def plain(eng, b):
            if not isinstance(b, int):
                eng.sem_inc(s_passed[eng.engine], 1)

        def either(eng, one):
            def run(b, ssm=False, **parts):
                if not ssm:
                    one(b, **parts)
                    return
                eng.wait_ge(s_flag, b + 1)
                plain(eng, b)
                flag = eng.value_load(careful_i[0:1, 0:1], min_val=0, max_val=2 * P)
                with eng.If(flag > 0):
                    one(b, ssm=True, careful=True, **parts)
                with eng.Else():
                    one(b, ssm=True, **parts)
            return run

        def passes(eng, one):
            one(-1, pre=True)
            one(0, pre=True, ssm=True)
            one(1, pre=True, ssm=True, before=True, post=True)
            one(2, pre=True, ssm=True, before=True, post=True, ffn=True)
            with eng.Fori(3, B - 1) as b:
                one(b, pre=True, ssm=True, before=True, post=True, ffn=True)
            one(B - 1, ssm=True, before=True, post=True, ffn=True)
            one(B, before=True, post=True, ffn=True)
            one(B + 1, ffn=True)

        def rows(b, t):
            return bass.ds(b * L + t * P, P)

        @block.sync
        def _(sp):
            sp.dma_start(id_i[:, :], ids).then_inc(s_ids, 16)
            sp.dma_start(row_i[:, 0:TRAIN], train_row.partition_broadcast(P)).then_inc(s_ids, 16)
            sp.dma_start(id_now[0:TRAIN, 0:1], train_col).then_inc(s_ids, 16)
            sp.dma_start(deltas, delta_t).then_inc(s_const, 16)
            sp.dma_start(dp_row[:, 0:H], Dp.partition_broadcast(P)).then_inc(s_const, 16)
            sp.dma_start(wr_row[:, :], Wr.partition_broadcast(P)).then_inc(s_const, 16)
            sp.dma_start(b2_row[:, :], b2.partition_broadcast(P)).then_inc(s_const, 16)
            sp.dma_start(a_t[:, :], A_t).then_inc(s_const, 16)
            sp.dma_start(b1s[:, :], b1_t).then_inc(s_const, 16)
            sp.dma_start(br_c, br.partition_broadcast(P)).then_inc(s_const, 16)
            sp.dma_start(q_gate[0:1, 0, :], bg).then_inc(s_const, 16)
            sp.dma_start(q_gate[BLK:BLK + 1, 0, :], bg).then_inc(s_const, 16)
            wx_v = Wx.rearrange("(k p) n -> p k n", p=P)
            wx_st = ffn_w[:, :, :].rearrange("p a b -> p (a b)")[:, 0:KC * PROJ].rearrange("p (k n) -> p k n", k=KC)
            sp.dma_start(wx_st[:, :, 0:2 * N + H], wx_v).then_inc(s_wload, 16)
            sp.dma_start(wx_st[:, :, 2 * N + H:PROJ], wx_v[:, :, 2 * N:2 * N + H]).then_inc(s_wload, 16)
            sp.dma_start(x[:, 1, 0:2, :].rearrange("p a (b n) -> p (a b) n", n=DM),
                         Wg.rearrange("(k p) n -> p k n", p=P)).then_inc(s_wload, 16)
            sp.dma_start(x[:, 1, 2:4, :].rearrange("p a (b n) -> p (a b) n", n=DM),
                         Wo.rearrange("(k p) n -> p k n", p=P)).then_inc(s_wload, 16)
            sp.wait_ge(s_stage, 1)
            sp.dma_start(adapted_dram, adapted).then_inc(s_ta, 16)

            w1_v = W1.rearrange("(k p) n -> p k n", p=P)
            w2_v = W2.rearrange("(f p) n -> p f n", p=P)

            def weights(b, c):
                if c < 2:
                    wait(sp, s_fo, b + 1)
                else:
                    wait(sp, s_ff, CHUNKS * b + c - 1)
                dst = ffn_w[:, c % 2, :]
                if c < HALF:
                    sp.dma_start(dst.rearrange("p (k n) -> p k n", k=KC), w1_v[:, :, 256 * c:256 * c + 256])\
                      .then_inc(s_w[c % 2], 16)
                else:
                    f = 2 * (c - HALF)
                    sp.dma_start(dst.rearrange("p (f n) -> p f n", f=2), w2_v[:, f:f + 2, :])\
                      .then_inc(s_w[c % 2], 16)

            def one(b, pre=False, ssm=False, before=False, post=False, ffn=False):
                if ffn:
                    weights(b - 2, 0)
                    weights(b - 2, 1)
                for h in range(H):
                    if ffn:
                        for c in range(2, CHUNKS):
                            if h == chunk_step(c - 2) + 1:
                                weights(b - 2, c)
                    if pre:
                        for p in range(TILES // 2):
                            if h == gather_step(p) + 2:
                                wait(sp, s_g2[p % 2], 32 * (2 * (b + 1) + p // 2 + 1))
                                for t in (2 * p, 2 * p + 1):
                                    sp.dma_start(h0_dram[rows(b + 1, t), :], emb[:, t % 4, :]).then_inc(s_hs[p % 2], 16)
                        for t in range(TILES):
                            n = TILES * (b + 1) + t
                            if h == pre_step(t) + 2:
                                wait(sp, s_xd, n + 1)
                                sp.dma_start(xd_dram[rows(b + 1, t), :], xn[:, t % 2, :]).then_inc(s_xs[t % 2], 16)
                            if h == pre_step(t) + 6:
                                wait(sp, s_gr, n + 1)
                                sp.dma_start(gate_dram[rows(b + 1, t), :], gate[:, t % 2, :]).then_inc(s_gs[t % 2], 16)
                    if post:
                        for t in range(TILES):
                            n = TILES * (b - 1) + t
                            half = 4 * (b - 1) + t // 2
                            if h == post_step(t) - 3:
                                wait(sp, s_xs[t % 2], 16 * (half + 1))
                                plain(sp, b)
                                wait(sp, s_gs[t % 2], 16 * (half + 1))
                                plain(sp, b)
                                wait(sp, s_yf, n)
                                plain(sp, b)
                                wait(sp, s_qt, n - 1)
                                plain(sp, b)
                                sp.dma_start(q_xd[:, 0, :], xd_dram[rows(b - 1, t), :]).then_inc(s_qx, 16)
                                sp.dma_start(q_gate[:, t % 2, :], gate_dram[rows(b - 1, t), :]).then_inc(s_ql[t % 2], 16)
                            if h == post_step(t) - 1:
                                wait(sp, s_hs[t // 2 % 2], 32 * (2 * (b - 1) + t // 4 + 1))
                                plain(sp, b)
                                wait(sp, s_store[t % 2], 32 * half)
                                plain(sp, b)
                                sp.dma_start(q_h[:, t % 2, :], h0_dram[rows(b - 1, t), :]).then_inc(s_qh[t % 2], 16)
                            if h == min(post_step(t) + 5, H - 1):
                                if t == 0:
                                    wait(sp, s_fx, 16 * (b - 1))
                                    plain(sp, b)
                                wait(sp, s_x2, n + 1)
                                sp.dma_start(xs_dram[P * t:P * t + P, :], x2[:, t % 2, :]).then_inc(s_store[t % 2], 16)
                                wait(sp, s_base, n + 1)
                                sp.dma_start(out[rows(b - 1, t), :], q_h[:, t % 2, :]).then_inc(s_store[t % 2], 16)
            passes(sp, one)
            sp.wait_ge(s_sc, 16 * (B + 1))
            for s in s_store:
                sp.wait_ge(s, 32 * 4 * B)

        @block.gpsimd
        def _(pool):
            pool.memset(ident[:, :], 0.0).then_inc(s_zero, 1)
            pool.memset(ones[:, :], 1.0).then_inc(s_zero, 1)
            pool.wait_ge(s_zero, 2)
            pool.affine_select(out=ident[:, :], in_=ident[:, :], compare_op=ALU.not_equal, fill=1.0, base=0,
                               pattern=[[-1, P]], channel_multiplier=1).then_inc(s_iota, 1)
            pool.affine_select(out=before[:, :], in_=ones[:, :], compare_op=ALU.is_gt, fill=0.0, base=0,
                               pattern=[[-1, P]], channel_multiplier=1).then_inc(s_iota, 1)
            pool.iota(slot_iota[:, :], pattern=[[1, P]], base=0, channel_multiplier=0,
                      allow_small_or_imprecise_dtypes=True).then_inc(s_iota, 1)
            pool.iota(token_no[:, :], pattern=[[P, TILES]], base=0, channel_multiplier=1,
                      allow_small_or_imprecise_dtypes=True).then_inc(s_iota, 1)
            pool.wait_ge(s_setup, 1)
            pool.indirect_dma_start(u[0:TRAIN, 3, 0:DM], None, W,
                                    bass.IndirectOffsetOnAxis(id_now[0:TRAIN, 0:1], 0)).then_inc(s_sc, 16)
            pool.wait_ge(s_setup, 3)
            pool.wait_ge(s_stage, 1)
            pool.wait_ge(s_ta, 16)

            def gather(b, p):
                wait(pool, s_hs[p % 2], 32 * (2 * b + p // 2))
                wait(pool, s_xn, TILES * b + 2 * p - 2)
                plain(pool, b)
                for t in (2 * p, 2 * p + 1):
                    pool.indirect_dma_start(emb[:, t % 4, :], None, W,
                                            bass.IndirectOffsetOnAxis(id_now[:, t:t + 1], 0)).then_inc(s_g1[p % 2], 16)

            def overlay(b, p):
                wait(pool, s_g1[p % 2], 32 * (2 * b + p // 2 + 1))
                plain(pool, b)
                for t in (2 * p, 2 * p + 1):
                    pool.indirect_dma_start(emb[:, t % 4, :], None, adapted_dram,
                                            bass.IndirectOffsetOnAxis(row_now[:, t:t + 1], 0),
                                            bounds_check=TRAIN - 1, oob_is_err=False).then_inc(s_g2[p % 2], 16)

            def one(b, pre=False, ssm=False, before=False, post=False, ffn=False):
                if pre:
                    wait(pool, s_g2[1], 32 * 2 * (b + 1))
                    wait(pool, s_g2[0], 32 * 2 * (b + 1))
                    plain(pool, b)
                    col = bass.ds((b + 1) * TILES, TILES)
                    pool.tensor_copy(id_now[:, :], id_i[:, col]).then_inc(s_idn, 1)
                    pool.tensor_copy(row_now[:, :], row_i[:, col]).then_inc(s_idn, 1)
                    pool.wait_ge(s_idn, 2 * (b + 1) + 2)
                for h in range(H):
                    if ssm:
                        i = H * b + h
                        wait(pool, s_d, i + 1)
                        if h % GROUP == 0:
                            wait(pool, s_y, 2 * (GROUPS * b + h // GROUP - 1))
                        pool.tensor_tensor(x[:, h // GROUP % 2, h % GROUP, :], u[:, h % USLOTS, :], u[:, h % USLOTS, :],
                                           ALU.mult).then_inc(s_x, 1)
                    if pre:
                        for p in range(TILES // 2):
                            if h == gather_step(p):
                                gather(b + 1, p)
                            if h == gather_step(p) + 1:
                                overlay(b + 1, p)
                        for t in range(TILES):
                            n = TILES * (b + 1) + t
                            if h == pre_step(t) + 1:
                                wait(pool, s_pt, n + 1)
                                pool.tensor_tensor(xn[:, t % 2, :], xn[:, t % 2, :], dp_row[:, :], ALU.mult).then_inc(s_xd, 1)
                    if post and h == 5:
                        wait(pool, s_yr, 2 * GROUPS * b)
                        wait(pool, s_ym, TILES * (b - 1))
                        plain(pool, b)
                        pool.tensor_copy(y_now[:, :, :], y_next[:, :, :]).then_inc(s_yn, 1)
                    if post:
                        for t in range(TILES):
                            n = TILES * (b - 1) + t
                            half = 4 * (b - 1) + t // 2
                            if h == max(post_step(t) - 2, 5):
                                wait(pool, s_qx, 16 * (n + 1))
                                wait(pool, s_yn, b)
                                g = q_xd[:, 0, :].rearrange("p (h d) -> p h d", d=HD)
                                pool.tensor_tensor(g, g, y_now[:, t, :].unsqueeze(2).broadcast_to([P, H, HD]),
                                                   ALU.add).then_inc(s_ym, 1)
                                wait(pool, s_ql[t % 2], 16 * (half + 1))
                                wait(pool, s_ym, n + 1)
                                pool.tensor_tensor(q_gate[:, t % 2, :], q_gate[:, t % 2, :], q_xd[:, 0, :],
                                                   ALU.mult).then_inc(s_yf, 1)
                            if h == min(post_step(t) + 5, H - 1):
                                wait(pool, s_x2, n + 1)
                                pool.tensor_tensor(q_h[:, t % 2, :], q_h[:, t % 2, :], x2[:, t % 2, :], ALU.add).then_inc(s_base, 1)
                    if ffn and h == FX_STEP:
                        wait(pool, s_ix, b - 1)
                        wait(pool, s_store[0], 128 * (b - 1))
                        wait(pool, s_store[1], 128 * (b - 1))
                        wait(pool, s_fo, b - 1)
                        wait(pool, s_sc, 16 * (b - 1))
                        plain(pool, b)
                        pool.indirect_dma_start(fx[:, :], None, xs_dram,
                                                bass.IndirectOffsetOnAxis(idx[:, 0:1], 0)).then_inc(s_fx, 16)
                        pool.tensor_copy(idx_out[:, :], idx[:, 1:2]).then_inc(s_ic, 1)
                        pool.tensor_copy(slot_w_now[:, :], slot_w[:, :]).then_inc(s_ic, 1)
                    if ffn and h == chunk_step(CHUNKS - 1) + 3:
                        wait(pool, s_fo, b)
                        plain(pool, b)
                        pool.indirect_dma_start(out, bass.IndirectOffsetOnAxis(idx_out[:, 0:1], 0), fx[:, :], None,
                                                compute_op=ALU.add)\
                            .then_inc(s_sc, 16)

            passes(pool, one)

        @block.scalar
        def _(act):
            act.preload_act_table_set(NATURAL_LOG_EXP)
            act.wait_ge(s_split, 1)

            def one(b, pre=False, ssm=False, before=False, post=False, ffn=False, careful=False):
                if ssm:
                    factor = ACT.Copy if careful else ACT.Exp
                    wait(act, s_pe, TILES * (b + 1))
                    act.activation(db_raw[:, :], db_raw[:, :], factor).then_inc(s_dbx, 1)
                    wait(act, s_dbx, b + 1)
                    wait(act, s_bc, 2 * H * b)
                    act.activation(edb[:, :], db_raw[:, :], ACT.Copy).then_inc(s_dbh, 1)
                    wait(act, s_u, 2 * H * b)
                    act.activation(eb[:, :], br_raw[:, :], factor).then_inc(s_eb, 1)

                def decay(h):
                    i = H * b + h
                    wait(act, s_d, i + 1)
                    wait(act, s_scan, i - 1)
                    act.activation(a[:, h % ASLOTS, :], u[:, h % USLOTS, :], ACT.Exp, scale=a_t[:, h:h + 1]).then_inc(s_a, 1)

                for h in range(H):
                    if pre:
                        for t in range(TILES):
                            n = TILES * (b + 1) + t
                            cols = slice(P * t, P * t + P)
                            if h == pre_step(t) + 2:
                                wait(act, s_pp, n + 1)
                                act.activation(proj[:, :], ps_p[:, 0:PROJ], ACT.Copy).then_inc(s_pj, 1)
                            if h == pre_step(t) + 3:
                                wait(act, s_pb, n + 1)
                                if t == 0:
                                    wait(act, s_eb, b + 1)
                                    wait(act, s_edb, b + 1)
                                    wait(act, s_cc, b + 1)
                                act.activation(br_raw[:, cols], ps_p[:, 0:P], ACT.Copy)
                                act.activation(c_raw[:, cols], ps_p[:, P:2 * P], ACT.Copy)
                                act.activation(db_raw[:, cols], ps_p[0:2 * H, 2 * P:3 * P], ACT.Copy).then_inc(s_pe, 1)
                            if h == pre_step(t) + 3:
                                wait(act, s_pg, n + 1)
                                wait(act, s_gs[t % 2], 16 * (4 * (b + 1) + t // 2))
                                act.activation(gate[:, t % 2, :], ps_t[:, :], ACT.Exp, scale=-1.0).then_inc(s_ge, 1)
                    if ffn:
                        for c in range(0, HALF, 2):
                            if h == chunk_step(c + 1) + 1:
                                wait(act, s_ff, CHUNKS * (b - 2) + c + 2)
                                for f in range(2 * c, 2 * c + 4):
                                    last = act.activation(hid[:, f, :], ps_f[:, P * (f % 4):P * (f % 4) + P], ACT.Identity,
                                                          bias=b1s[:, f:f + 1])
                                last.then_inc(s_hc, 1)
                    if ffn:
                        if 1 <= h <= 2:
                            wait(act, s_lb, 2 * (b - 2) + h)
                            act.activation(logit_row[:, 4 * h - 4:4 * h, :].rearrange("p k n -> p (k n)"), ps_f[:, :],
                                           ACT.Copy).then_inc(s_lr, 1)
                        if h == 3:
                            wait(act, s_rmax, b - 1)
                            act.activation(weigh[:, 0, :], logit[:, :], ACT.Exp, bias=small[:, 2:3]).then_inc(s_re, 1)
                    if ssm:
                        wait(act, s_u, 2 * (H * b + h + 1))
                        if careful:
                            part = a[:, h % ASLOTS, :]
                            wait(act, s_scan, H * b + h - 1)
                            act.activation(part, u[:, h % USLOTS, :], ACT.Abs).then_inc(s_abs, 1)
                            wait(act, s_abs, 2 * (H * b + h) + 1)
                            act.activation(part, part, ACT.Exp, scale=-1.0).then_inc(s_abs, 1)
                            wait(act, s_abs, 2 * (H * b + h) + 2)
                            act.activation(part, part, ACT.Ln, bias=1.0).then_inc(s_l1, 1)
                            wait(act, s_sp, H * b + h + 1)
                            act.sem_inc(s_d, 1)
                        else:
                            act.activation(u[:, h % USLOTS, :], u[:, h % USLOTS, :], ACT.Ln, bias=1.0).then_inc(s_d, 1)
                    if pre:
                        for t in range(TILES):
                            n = TILES * (b + 1) + t
                            if h == pre_step(t):
                                wait(act, s_pt, n + 1)
                                wait(act, s_pg, n)
                                act.activation(xt_hi[:, :, :].rearrange("p k n -> p (k n)"), ps_t[:, :], ACT.Copy).then_inc(s_xth, 1)
                    if post:
                        for t in range(TILES):
                            n = TILES * (b - 1) + t
                            if h == post_step(t):
                                wait(act, s_qt, n + 1)
                                wait(act, s_wo, n)
                                act.activation(yt_hi[:, :, :].rearrange("p k n -> p (k n)"), ps_b[:, :], ACT.Copy).then_inc(s_yth, 1)
                    if ssm:
                        if h:
                            decay(h - 1)
                        if h == 5:
                            wait(act, s_y, 2 * GROUPS * b)
                            act.activation(cc[:, :], c_raw[:, :], ACT.Copy).then_inc(s_cc, 1)
                    if pre:
                        for p in range(TILES // 2):
                            if h == gather_step(p) + 3:
                                n = 4 * (b + 1) + p
                                q = 2 * (p % 2)
                                wait(act, s_mv, 2 * n + 2)
                                act.activation(rstd[:, q:q + 2], mv[:, q:q + 2, 1], ACT.Ln, bias=eps_c).then_inc(s_ln, 1)
                                wait(act, s_ln, n + 1)
                                act.activation(rstd[:, q:q + 2], rstd[:, q:q + 2], ACT.Exp, scale=-0.5).then_inc(s_rs, 1)
                        for t in range(TILES):
                            n = TILES * (b + 1) + t
                            if h == pre_step(t) + 5:
                                wait(act, s_gm, n + 1)
                                act.activation(gate[:, t % 2, :], gate[:, t % 2, :], ACT.Ln, bias=1.0).then_inc(s_gl, 1)
                                wait(act, s_gl, n + 1)
                                act.activation(gate[:, t % 2, :], gate[:, t % 2, :], ACT.Exp, scale=-1.0).then_inc(s_gr, 1)
                    if post:
                        for t in range(TILES):
                            n = TILES * (b - 1) + t
                            if h == post_step(t) + 3:
                                wait(act, s_mv2, n + 1)
                                q = t % 2
                                act.activation(rstd2[:, q:q + 1], mv2[:, q, 1:2], ACT.Ln, bias=eps_c).then_inc(s_ln2, 1)
                                wait(act, s_ln2, n + 1)
                                act.activation(rstd2[:, q:q + 1], rstd2[:, q:q + 1], ACT.Exp, scale=-0.5).then_inc(s_rs2, 1)
                    if ffn:
                        if h == FX_STEP + 1:
                            wait(act, s_ft, b - 1)
                            act.activation(fxt[:, :, :].rearrange("p k n -> p (k n)"), ps_f[:, :], ACT.Copy).then_inc(s_fxt, 1)
                        if h == chunk_step(HALF) - 1:
                            wait(act, s_hc, HALF // 2 * (b - 1))
                            act.activation(hid[:, :, :], hid[:, :, :], ACT.Gelu).then_inc(s_gelu, 1)
                            act.preload_act_table_set(NATURAL_LOG_EXP)
                if ssm:
                    decay(H - 1)
                if ssm and not careful:
                    act.sem_inc(s_abs, 2 * H)
                    act.sem_inc(s_l1, H)

            passes(act, either(act, one))

        @block.tensor
        def _(pe):
            pe.wait_ge(s_setup, 2)
            pe.wait_ge(s_const, 16 * 9)
            pe.matmul(ps_b[0:TRAIN, :], one_hot[0:TRAIN, 0, 0:TRAIN], deltas, start=True, stop=True)\
              .then_inc(s_tm, 1)
            pe.wait_ge(s_split, 1)

            def split_product(psum, lhs_hi, lhs_lo, rhs_hi, rhs_lo, more=False):
                parts = [(lhs_hi, rhs_hi), (lhs_lo, rhs_hi), (lhs_hi, rhs_lo)]
                for k in range(KC):
                    for j, (lhs, rhs) in enumerate(parts):
                        last = pe.matmul(psum, lhs[:, k, :], rhs[:, k, :], start=(k == 0 and j == 0),
                                         stop=(k == KC - 1 and j == 2 and not more))
                return last

            def one(b, pre=False, ssm=False, before=False, post=False, ffn=False):
                def broadcast(h):
                    if h == 0:
                        wait(pe, s_edb, b + 1)
                    for half in range(2):
                        k = 2 * h + half
                        if k < RING:
                            wait(pe, s_u, 2 * H * b)
                        else:
                            wait(pe, s_u, 2 * H * b + k - RING + 1)
                        pe.matmul(ps_e[:, k % RING, :], head_sel[:, h:h + 1].broadcast_to([2 * H, P]),
                                  edb[:, DM * half:DM * half + DM], start=True, stop=True).then_inc(s_bc, 1)

                def contract(c, g, half):
                    n = 2 * (GROUPS * c + g) + half
                    wait(pe, s_scan, H * c + GROUP * (g + 1))
                    wait(pe, s_pick, n)
                    if g == 0:
                        wait(pe, s_cc, c + 1)
                    for k in range(16 * half, 16 * half + 16):
                        q, j = k % 4, k // 4 % 4
                        last = pe.matmul(ps_y[BLK * q:BLK * q + BLK, P * j:P * j + P],
                                         cc[:, BLK * k:BLK * k + BLK],
                                         x[:, g % 2, :, BLK * k:BLK * k + BLK], start=True, stop=True,
                                         tile_position=(0, BLK * q))
                    last.then_inc(s_y, 1)

                if ssm:
                    broadcast(0)
                for h in range(H):
                    if ssm and h + 1 < H:
                        broadcast(h + 1)
                    g, left = h // GROUP - 1, h % GROUP
                    if left == 2 and (ssm if g >= 0 else before):
                        contract(b if g >= 0 else b - 1, g % GROUPS, 0)
                    if pre:
                        for t in range(TILES):
                            n = TILES * (b + 1) + t
                            if h == pre_step(t):
                                wait(pe, s_xn, n + 1)
                                wait(pe, s_ge, n)
                                for k in range(KC):
                                    last = pe.transpose(ps_t[:, P * k:P * k + P], xn[:, t % 2, P * k:P * k + P], ident[:, :])
                                last.then_inc(s_pt, 1)
                    if post:
                        for t in range(TILES):
                            n = TILES * (b - 1) + t
                            if h == post_step(t):
                                wait(pe, s_yf, n + 1)
                                wait(pe, s_h1, n)
                                for k in range(KC):
                                    last = pe.transpose(ps_b[:, P * k:P * k + P], q_gate[:, t % 2, P * k:P * k + P], ident[:, :])
                                last.then_inc(s_qt, 1)
                    if pre and h == FLAG_STEP + 1:
                        wait(pe, s_ind, b + 2)
                        pe.matmul(ps_p[0:1, 0:2], ones[:, 0:1], unsafe[:, 2:4], start=True, stop=True).then_inc(s_cnt, 1)
                    if left == 3 and (ssm if g >= 0 else before):
                        contract(b if g >= 0 else b - 1, g % GROUPS, 1)
                    if pre:
                        for t in range(TILES):
                            n = TILES * (b + 1) + t
                            if h == pre_step(t) + 1:
                                wait(pe, s_xtl, n + 1)
                                wait(pe, s_pe, n)
                                split_product(ps_p[:, 0:PROJ], xt_hi, xt_lo, wx_hi, wx_lo).then_inc(s_pp, 1)
                            if h == pre_step(t) + 2:
                                split_product(ps_t[:, :], xt_hi, xt_lo, wg_hi, wg_lo, more=True)
                                pe.matmul(ps_t[:, :], ones_r[:, :], bias_g[:, :], start=False, stop=True).then_inc(s_pg, 1)
                                wait(pe, s_pj, n + 1)
                                for k, width in enumerate((N, N, 2 * H)):
                                    last = pe.transpose(ps_p[0:width, P * k:P * k + P], proj[:, P * k:P * k + width], ident[:, :])
                                last.then_inc(s_pb, 1)
                    if post:
                        for t in range(TILES):
                            n = TILES * (b - 1) + t
                            if h == post_step(t) + 1:
                                if isinstance(b, int) and b == 1 and t == 0:
                                    wait(pe, s_wsplit, 2)
                                wait(pe, s_ytl, n + 1)
                                split_product(ps_b[:, :], yt_hi, yt_lo, wo_hi, wo_lo).then_inc(s_wo, 1)
                    if ffn:
                        if h < 2:
                            if h == 0:
                                wait(pe, s_dg, b - 1)
                                wait(pe, s_ol, b - 1)
                            else:
                                wait(pe, s_lr, 2 * (b - 2) + 1)
                            pe.matmul(ps_f[:, :], ones[:, :], one_hot[:, 4 * h:4 * h + 4, :], start=True, stop=True)\
                              .then_inc(s_lb, 1)
                        if h == 4:
                            wait(pe, s_es, b - 1)
                            wait(pe, s_lr, 2 * (b - 1))
                            pe.matmul(ps_f[:, 0:1], ones[:, :], weigh[:, 3, 0:1], start=True, stop=True).then_inc(s_z, 1)
                        if h == 5:
                            wait(pe, s_rv, b - 1)
                            wait(pe, s_oh, b - 1)
                            for t in range(TILES):
                                last = pe.matmul(ps_f[:, 2:6], one_hot[:, t, :], slot_rhs[:, t, :], start=(t == 0), stop=(t == TILES - 1))
                            last.then_inc(s_sl, 1)
                        if h == FX_STEP + 1:
                            wait(pe, s_fx, 16 * (b - 1))
                            wait(pe, s_ix, b - 1)
                            for k in range(KC):
                                last = pe.transpose(ps_f[:, P * k:P * k + P], fx[:, P * k:P * k + P], ident[:, :])
                            last.then_inc(s_ft, 1)
                        for c in range(CHUNKS):
                            if h == chunk_step(c):
                                wait(pe, s_w[c % 2], 16 * (HALF * (b - 2) + c // 2 + 1))
                                if c < HALF:
                                    if c < 2:
                                        wait(pe, s_fxt, b - 1)
                                    else:
                                        wait(pe, s_hc, HALF // 2 * (b - 2) + c // 2)
                                    w = ffn_w[:, c % 2, :].rearrange("p (k n) -> p k n", k=KC)
                                    for f in range(2):
                                        col = P * (2 * (c % 2) + f)
                                        for k in range(KC):
                                            last = pe.matmul(ps_f[:, col:col + P], w[:, k, P * f:P * f + P], fxt[:, k, :],
                                                             start=(k == 0), stop=(k == KC - 1))
                                else:
                                    wait(pe, s_gelu, b - 1)
                                    w = ffn_w[:, c % 2, :].rearrange("p (f n) -> p f n", f=2)
                                    for j in range(2):
                                        f = 2 * (c - HALF) + j
                                        last = pe.matmul(ps_f[:, :], hid[:, f, :], w[:, j, :], start=(f == 0), stop=(f == FT - 1))
                                last.then_inc(s_ff, 1)

            passes(pe, one)

        @block.vector
        def _(dve):
            n_link = [0]

            def link(ins):
                n_link[0] += 1
                ins.then_inc(s_r, 1)
                dve.wait_ge(s_r, n_link[0])

            dve.memset(eps_c, EPS)
            link(dve.memset(small[:, 4:5], 0.0))
            dve.wait_ge(s_ids, 48)
            tr_f, tc_f, wrap = rank[:, :, :].rearrange("p a b -> p (a b)"), small[0:TRAIN, 8:9], small[0:TRAIN, 9:10]
            wrap_ids = y_next[:, 0:2, :].rearrange("p a b -> p (a b)")
            for src, dst, tmp in ((id_i[:, :], id_f[:, :], wrap_ids), (row_i[:, :], tr_f, wrap_ids),
                                  (id_now[0:TRAIN, 0:1], tc_f, wrap)):
                link(dve.tensor_copy(dst, src))
                link(dve.tensor_scalar(tmp, dst, 0.0, float(VOCAB), ALU.is_lt, ALU.mult))
                link(dve.tensor_tensor(dst, dst, tmp, ALU.add))
            link(dve.tensor_scalar(id_f[:, :], id_f[:, :], 0.0, float(VOCAB - 1), ALU.max, ALU.min))
            link(dve.tensor_copy(id_i[:, :], id_f[:, :]))
            link(dve.tensor_scalar(wrap, tc_f, 0.0, float(VOCAB - 1), ALU.max, ALU.min))
            dve.tensor_copy(id_now[0:TRAIN, 0:1], wrap).then_inc(s_setup, 1)
            dve.wait_ge(s_iota, 4)
            dve.tensor_scalar(one_hot[0:TRAIN, 0, 0:TRAIN], tr_f[0:TRAIN, :], tc_f, None, ALU.is_equal).then_inc(s_setup, 1)
            eq = x[:, 0, :, :].rearrange("p a b -> p (a b)").rearrange("p (t j) -> p t j", j=TRAIN)
            link(dve.tensor_tensor(eq, id_f[:, :].unsqueeze(2).broadcast_to([P, B * TILES, TRAIN]),
                                   tr_f.unsqueeze(1).broadcast_to([P, B * TILES, TRAIN]), ALU.is_equal))
            link(dve.tensor_scalar(wrap_ids, slot_iota[:, 0:TRAIN], -1.0, float(TRAIN), ALU.mult, ALU.add))
            link(dve.tensor_tensor(eq, eq, wrap_ids.unsqueeze(1).broadcast_to([P, B * TILES, TRAIN]), ALU.mult))
            link(dve.tensor_reduce(id_f[:, :], eq, axis=AX.X, op=ALU.max))
            link(dve.tensor_scalar(id_f[:, :], id_f[:, :], -1.0, float(TRAIN), ALU.mult, ALU.add))
            dve.tensor_copy(row_i[:, :], id_f[:, :]).then_inc(s_setup, 1)
            dve.wait_ge(s_sc, 16)
            dve.wait_ge(s_tm, 1)
            dve.tensor_tensor(adapted, u[0:TRAIN, 3, 0:DM], ps_b[0:TRAIN, :], ALU.add).then_inc(s_stage, 1)
            dve.sem_inc(s_fo, 1)
            dve.sem_inc(s_ol, 1)
            dve.wait_ge(s_wload, 64)
            dve.wait_ge(s_const, 144)
            wx_st = ffn_w[:, :, :].rearrange("p a b -> p (a b)")[:, 0:KC * PROJ].rearrange("p (k n) -> p k n", k=KC)
            wg_st = x[:, 1, 0:2, :].rearrange("p a (b n) -> p (a b) n", n=DM)
            wo_st = x[:, 1, 2:4, :].rearrange("p a (b n) -> p (a b) n", n=DM)
            dve.tensor_copy(wx_hi[:, :, :], wx_st)
            link(dve.tensor_copy(wg_hi[:, :, :], wg_st))
            dve.tensor_tensor(wx_lo[:, :, :], wx_st, wx_hi[:, :, :].bitcast(F32), ALU.subtract)
            link(dve.tensor_tensor(wg_lo[:, :, :], wg_st, wg_hi[:, :, :].bitcast(F32), ALU.subtract))
            link(dve.tensor_reduce(diag32[:, :], ident[:, :].rearrange("p (g c) -> p c g", c=BLK), axis=AX.X, op=ALU.add))
            link(dve.tensor_copy(head_sel[:, :], diag32[0:2 * H, :]))
            link(dve.tensor_copy(ones_r[:, :], ones[0:2 * BLK, :]))
            link(dve.tensor_copy(x2[:, 0, 0:H], dp_row[:, 0:H]))
            link(dve.tensor_copy(dp_row[:, :].rearrange("p (h d) -> p h d", d=HD),
                                 x2[:, 0, 0:H].unsqueeze(2).broadcast_to([P, H, HD])))
            link(dve.memset(slot_rhs[:, :, 3], 0.0))
            link(dve.memset(unsafe[:, :], 0.0))
            link(dve.tensor_copy(slot_rhs[:, :, 0], token_no[:, :]))
            link(dve.memset(x2[0:2 * BLK, 1, :], 0.0))
            link(dve.tensor_copy(bias_g[:, :], x2[0:2 * BLK, 1, :]))
            link(dve.tensor_copy(bias_g[0:1, :], q_gate[0:1, 0, :]))
            link(dve.tensor_copy(bias_g[BLK:BLK + 1, :], q_gate[BLK:BLK + 1, 0, :]))
            link(dve.tensor_tensor(x2[BLK:BLK + 1, 0, :], q_gate[BLK:BLK + 1, 0, :], bias_g[BLK:BLK + 1, :].bitcast(F32), ALU.subtract))
            link(dve.tensor_copy(bias_g[BLK:BLK + 1, :], x2[BLK:BLK + 1, 0, :]))
            dve.memset(small[:, 4:5], 0.0).then_inc(s_split, 1)

            links = n_link[0]
            RANKS = [(0, 2), (2, 5), (5, 8)]
            CHAIN = 3 + (TILES - 1) + 2 * TILES + 7

            def router(b, step, count):
                def chain(ins):
                    count[0] += 1
                    ins.then_inc(s_r, 1)

                def chained():
                    dve.wait_ge(s_r, links + CHAIN * b + count[0])

                flat = logit_row[:, :, :].rearrange("p k n -> p (k n)")
                if step == 0:
                    dve.wait_ge(s_lg, TILES * (b + 1))
                    dve.tensor_tensor(one_hot[:, :, :], ident[:, :].unsqueeze(1).broadcast_to([P, TILES, P]),
                                      logit[:, :].unsqueeze(2).broadcast_to([P, TILES, P]), ALU.mult).then_inc(s_dg, 1)
                    for q in (0, 3):
                        chain(dve.memset(rank[:, q, :], 0.0))
                if step == 2:
                    dve.wait_ge(s_lr, 2 * b + 2)
                    chain(dve.tensor_reduce(small[:, 3:4], flat, axis=AX.X, op=ALU.max))
                    chained()
                    dve.tensor_scalar(small[:, 2:3], small[:, 3:4], -1.0, None, ALU.mult).then_inc(s_rmax, 1)
                if 2 <= step <= 4:
                    junk = one_hot[:, :, :].rearrange("p t c -> p (t c)")
                    for t in range(*RANKS[step - 2]):
                        mine = logit[:, t:t + 1]
                        row = lambda lo, hi: flat[:, P * lo:P * hi]
                        chained()
                        if t:
                            chain(dve.tensor_scalar(junk[:, 0:P * t], row(0, t), mine, 0.0, ALU.is_ge, ALU.add,
                                                    accum_out=rank[:, 0, t:t + 1]))
                            chained()
                        chain(dve.tensor_scalar(junk[:, 0:P * (TILES - t)], row(t, TILES), mine, 0.0, ALU.is_gt, ALU.add,
                                                accum_out=rank[:, 1, t:t + 1]))
                        chained()
                        chain(dve.scalar_tensor_tensor(junk[:, 0:P], row(t, t + 1), mine, before[:, :], ALU.is_equal, ALU.mult,
                                                       accum_out=rank[:, 2, t:t + 1]))
                if step == 4:
                    chained()
                    chain(dve.tensor_tensor(rank[:, 4, :], rank[:, 0, :], rank[:, 1, :], ALU.add))
                    chained()
                    chain(dve.tensor_tensor(rank[:, 5, :], rank[:, 4, :], rank[:, 2, :], ALU.add))
                    chained()
                    chain(dve.tensor_scalar(weigh[:, 1, :], rank[:, 5, :], float(KEEP), None, ALU.is_lt))
                    dve.wait_ge(s_re, b + 1)
                    chained()
                    chain(dve.tensor_tensor(weigh[:, 2, :], weigh[:, 0, :], weigh[:, 1, :], ALU.mult))
                    chained()
                    dve.tensor_reduce(weigh[:, 3, 0:1], weigh[:, 2, :], axis=AX.X, op=ALU.add).then_inc(s_es, 1)
                if step == 5:
                    for t in range(TILES):
                        last = dve.tensor_scalar(one_hot[:, t, :], slot_iota[:, :], rank[:, 5, t:t + 1], None, ALU.is_equal)
                    last.then_inc(s_oh, 1)
                    chain(dve.tensor_copy(slot_rhs[:, :, 1], token_no[:, :]))
                    dve.wait_ge(s_z, b + 1)
                    chain(dve.reciprocal(small[:, 5:6], ps_f[:, 0:1]))
                    chained()
                    dve.tensor_scalar(slot_rhs[:, :, 2], weigh[:, 2, :], small[:, 5:6], None, ALU.mult).then_inc(s_rv, 1)
                    chain(dve.tensor_scalar(token_no[:, :], token_no[:, :], float(L), None, ALU.add))
                if step == 6:
                    dve.wait_ge(s_sl, b + 1)
                    dve.tensor_copy(slot_w[:, :], ps_f[:, 4:5]).then_inc(s_sw, 1)
                    dve.tensor_copy(idx[:, :], ps_f[:, 2:4]).then_inc(s_ix, 1)
                    assert count[0] == CHAIN, count

            def one(b, pre=False, ssm=False, before=False, post=False, ffn=False, careful=False):
                def scan(c, h):
                    i = H * c + h
                    s = x[:, h // GROUP % 2, h % GROUP, :]
                    wait(dve, s_a, i + 1)
                    wait(dve, s_x, i + 1)
                    dve.tensor_tensor_scan(s, a[:, h % ASLOTS, :], s, 0.0, ALU.mult, ALU.add).then_inc(s_scan, 1)

                if before:
                    scan(b - 1, H - 2)
                if ssm:
                    wait(dve, s_dbh, b + 1)
                    dve.tensor_tensor(edb[H:2 * H, :], db_raw[H:2 * H, :], edb[H:2 * H, :].bitcast(F32), ALU.subtract)\
                       .then_inc(s_edb, 1)

                def pick(c, g, half):
                    n = 2 * (GROUPS * c + g) + half
                    wait(dve, s_y, n + 1)
                    wait(dve, s_yr, n)
                    v = "p (b c) -> p b c"
                    dve.tensor_tensor(picked[:, :].rearrange(v, c=BLK), ps_y[:, :].rearrange(v, c=BLK),
                                      diag32[:, :].unsqueeze(1).broadcast_to([P, DM // BLK, BLK]), ALU.mult).then_inc(s_pick, 1)
                    wait(dve, s_pick, n + 1)
                    if g == 0:
                        wait(dve, s_yn, c)
                    dve.tensor_reduce(y_next[:, 4 * half:4 * half + 4, GROUP * g:GROUP * g + GROUP],
                                      picked[:, :].rearrange("p (t h c) -> p t h c", h=GROUP, c=BLK), axis=AX.X, op=ALU.add)\
                       .then_inc(s_yr, 1)

                if before:
                    scan(b - 1, H - 1)
                count = [0]
                for h in range(H):
                    if ssm:
                        i = H * b + h
                        if h == 0:
                            wait(dve, s_eb, b + 1)
                        wait(dve, s_a, i - USLOTS + 1)
                        wait(dve, s_x, i - USLOTS + 1)
                        for half in range(2):
                            cols = slice(DM * half, DM * half + DM)
                            wait(dve, s_bc, 2 * i + half + 1)
                            dve.tensor_tensor(u[:, h % USLOTS, cols], ps_e[:, (2 * h + half) % RING, :], eb[:, cols],
                                              ALU.add if careful else ALU.mult).then_inc(s_u, 1)
                    g, left = h // GROUP, h % GROUP
                    if left == 3 and (ssm if g >= 1 else before):
                        pick(b if g >= 1 else b - 1, (g - 1) % GROUPS, 0)
                    if pre:
                        for t in range(TILES):
                            n = TILES * (b + 1) + t
                            if h == pre_step(t) + 1:
                                wait(dve, s_xth, n + 1)
                                dve.tensor_tensor(xt_lo[:, :, :].rearrange("p k n -> p (k n)"), ps_t[:, :],
                                                  xt_hi[:, :, :].rearrange("p k n -> p (k n)").bitcast(F32), ALU.subtract).then_inc(s_xtl, 1)
                    if post:
                        for t in range(TILES):
                            n = TILES * (b - 1) + t
                            if h == post_step(t) + 1:
                                wait(dve, s_yth, n + 1)
                                dve.tensor_tensor(yt_lo[:, :, :].rearrange("p k n -> p (k n)"), ps_b[:, :],
                                                  yt_hi[:, :, :].rearrange("p k n -> p (k n)").bitcast(F32), ALU.subtract).then_inc(s_ytl, 1)
                    if h >= 2 and ssm:
                        scan(b, h - 2)
                    if careful:
                        wait(dve, s_l1, H * b + h + 1)
                        dve.scalar_tensor_tensor(u[:, h % USLOTS, :], u[:, h % USLOTS, :], 0.0, a[:, h % ASLOTS, :],
                                                 ALU.max, ALU.add).then_inc(s_sp, 1)
                    if left == 0 and (ssm if g >= 2 else before):
                        pick(b if g >= 2 else b - 1, (g - 2) % GROUPS, 1)
                    if ffn:
                        router(b - 2, h, count)
                    if pre:
                        for p in range(TILES // 2):
                            n = 4 * (b + 1) + p
                            if h == gather_step(p) + 3:
                                wait(dve, s_g2[p % 2], 32 * (2 * (b + 1) + p // 2 + 1))
                                for j in range(2):
                                    dve.bn_stats(stats[:, (2 * p + j) % 4, :], emb[:, (2 * p + j) % 4, :]).then_inc(s_st, 1)
                                for j in range(2):
                                    wait(dve, s_st, 2 * n + j + 1)
                                    plain(dve, b)
                                    dve.bn_aggr(mv[:, (2 * p + j) % 4, :], stats[:, (2 * p + j) % 4, :]).then_inc(s_mv, 1)
                        for t in range(TILES):
                            n = TILES * (b + 1) + t
                            if h == pre_step(t) - 1:
                                wait(dve, s_rs, 4 * (b + 1) + t // 2 + 1)
                                wait(dve, s_xs[t % 2], 16 * (4 * (b + 1) + t // 2))
                                dve.tensor_scalar(xn[:, t % 2, :], emb[:, t % 4, :], mv[:, t % 4, 0:1], rstd[:, t % 4:t % 4 + 1],
                                                  ALU.subtract, ALU.mult).then_inc(s_xn, 1)
                            if h == pre_step(t) + 4:
                                wait(dve, s_ge, n + 1)
                                dve.tensor_scalar(gate[:, t % 2, :], gate[:, t % 2, :], BIG, None, ALU.min).then_inc(s_gm, 1)
                    if post:
                        for t in range(TILES):
                            n = TILES * (b - 1) + t
                            q = t % 2
                            if h == post_step(t) + 2:
                                wait(dve, s_wo, n + 1)
                                wait(dve, s_qh[q], 16 * (4 * (b - 1) + t // 2 + 1))
                                dve.tensor_tensor(q_h[:, q, :], q_h[:, q, :], ps_b[:, :], ALU.add).then_inc(s_h1, 1)
                                wait(dve, s_h1, n + 1)
                                dve.bn_stats(stats2[:, q, :], q_h[:, q, :]).then_inc(s_st2, 1)
                                wait(dve, s_st2, n + 1)
                                plain(dve, b)
                                dve.bn_aggr(mv2[:, q, :], stats2[:, q, :]).then_inc(s_mv2, 1)
                            if h == min(post_step(t) + 4, H - 1):
                                wait(dve, s_rs2, n + 1)
                                wait(dve, s_store[q], 32 * (4 * (b - 1) + t // 2))
                                wait(dve, s_base, n - 1)
                                dve.tensor_scalar(x2[:, q, :], q_h[:, q, :], mv2[:, q, 0:1], rstd2[:, q:q + 1],
                                                  ALU.subtract, ALU.mult).then_inc(s_x2, 1)
                                wait(dve, s_x2, n + 1)
                                if t == 0:
                                    wait(dve, s_sl, b - 1)
                                wait(dve, s_lg, n)
                                dve.tensor_tensor_reduce(out=one_hot[:, 0:4, :].rearrange("p t c -> p (t c)"), in0=x2[:, q, :], in1=wr_row[:, :], scale=1.0,
                                                         scalar=br_c, op0=ALU.mult, op1=ALU.add,
                                                         accum_out=logit[:, t:t + 1]).then_inc(s_lg, 1)
                    if isinstance(b, int) and b == -1 and h == WO_STEP:
                        dve.tensor_copy(wo_hi[:, :, :], wo_st).then_inc(s_wsplit, 1)
                    if isinstance(b, int) and b == -1 and h == WO_STEP + 4:
                        dve.wait_ge(s_wsplit, 1)
                        dve.tensor_tensor(wo_lo[:, :, :], wo_st, wo_hi[:, :, :].bitcast(F32), ALU.subtract).then_inc(s_wsplit, 1)
                    if pre and h == FLAG_STEP:
                        wait(dve, s_pe, TILES * (b + 2))
                        dve.tensor_reduce(unsafe[:, 0:1], br_raw[:, :], axis=AX.X, op=ALU.max,
                                          apply_absolute_value=True).then_inc(s_mx, 1)
                        dve.tensor_reduce(unsafe[0:2 * H, 1:2], db_raw[:, :], axis=AX.X, op=ALU.max,
                                          apply_absolute_value=True).then_inc(s_mx, 1)
                        wait(dve, s_mx, 2 * (b + 2))
                        dve.tensor_scalar(unsafe[:, 2:4], unsafe[:, 0:2], SAFE, None, ALU.is_gt).then_inc(s_ind, 1)
                    if pre and h == FLAG_STEP + 2:
                        wait(dve, s_cnt, b + 2)
                        wait(dve, s_eb, b + 1)
                        dve.tensor_reduce(small[0:1, 6:7], ps_p[0:1, 0:2], axis=AX.X, op=ALU.add).then_inc(s_tot, 1)
                        wait(dve, s_tot, b + 2)
                        dve.tensor_copy(careful_i[0:1, 0:1], small[0:1, 6:7]).then_inc(s_flag, 1)
                    if ffn and h == chunk_step(CHUNKS - 1) + 1:
                        wait(dve, s_ff, CHUNKS * (b - 1))
                        wait(dve, s_ic, 2 * (b - 1))
                        dve.tensor_tensor(fx[:, :], ps_f[:, :], b2_row[:, :], ALU.add).then_inc(s_ol, 1)
                    if ffn and h == chunk_step(CHUNKS - 1) + 2:
                        wait(dve, s_ol, b)
                        dve.tensor_scalar(fx[:, :], fx[:, :], slot_w_now[:, 0:1], None, ALU.mult).then_inc(s_fo, 1)

                if ssm and not careful:
                    dve.sem_inc(s_sp, H)

            passes(dve, either(dve, one))


def kernel(**inputs):
    import numpy as np
    import concourse.bacc as bacc
    from concourse.bass_utils import run_bass_kernel_spmd

    g = {k: np.asarray(v) for k, v in inputs.items()}
    flat = lambda v: np.ascontiguousarray(v.reshape(1, -1))
    arrays = {
        "ids": np.ascontiguousarray(g["x"].reshape(B * TILES, P).T),
        "W": np.ascontiguousarray(g["L0_tok_W"]),
        "delta_t": np.ascontiguousarray(g["L0_tok_delta"].reshape(DM, TRAIN).T),
        "train_row": flat(g["L0_tok_token_indices"]),
        "train_col": np.ascontiguousarray(g["L0_tok_token_indices"].reshape(-1, 1)),
        "Wx": np.ascontiguousarray(g["L0_attn_Wx"]),
        "Wg": np.ascontiguousarray(g["L0_attn_Wg"]),
        "bg": flat(g["L0_attn_bg"]),
        "Wo": np.ascontiguousarray(g["L0_attn_Wo"]),
        "A_t": np.ascontiguousarray(g["L0_attn_A"].T),
        "Dp": flat(g["L0_attn_Dp"]),
        "Wr": flat(g["L0_ffn_Wr"]),
        "br": flat(g["L0_ffn_br"]),
        "W1": np.ascontiguousarray(g["L0_ffn_W1"]),
        "b1_t": np.ascontiguousarray(g["L0_ffn_b1"].reshape(FT, P).T),
        "W2": np.ascontiguousarray(g["L0_ffn_W2"]),
        "b2": flat(g["L0_ffn_b2"]),
    }
    nc = bacc.Bacc("TRN2", target_bir_lowering=False, num_devices=1)
    aps = {k: nc.dram_tensor(k, v.shape, mybir.dt.from_np(v.dtype), kind="ExternalInput").ap() for k, v in arrays.items()}
    out = nc.dram_tensor("out", [B * L, DM], F32, kind="ExternalOutput").ap()
    build(nc, out=out, **aps)
    r = run_bass_kernel_spmd(nc, [arrays], core_ids=[0])
    return r.results[0]["out"].reshape(B, L, DM)
```
